# Optimizing a Trainium2 kernel written in Bass

```python
import numpy as np
import jax
import jax.numpy as jnp

def _softmax(x, axis=-1):
    return jax.nn.softmax(x, axis=axis)

def _gelu(x):
    return jax.nn.gelu(x, approximate=True)

def _silu(x):
    return jax.nn.silu(x)

def _sigmoid(x):
    return jax.nn.sigmoid(x)

def _layernorm(x, axis=-1, eps=1e-05):
    m = jnp.mean(x, axis=axis, keepdims=True)
    v = jnp.var(x, axis=axis, keepdims=True)
    return (x - m) / jnp.sqrt(v + eps)

def _scatter_add(tgt, idx, src, axis=0):
    return tgt.at[idx].add(src)

def _segment_sum(src, seg, n):
    return jax.ops.segment_sum(src, seg, n)
kernel_name = 'mk_xattn_seq_d2_seqx_r4_78c51e'

def setup_inputs(seed: int=0):
    np.random.seed(seed)
    _w = jnp.asarray

    def _rec_inputs():
        import jax
        import jax.numpy as jnp
        _rk = jax.random.key(seed)
        x = 0.0003765 + 1 * jax.random.normal(jax.random.fold_in(_rk, 1), (8, 256, 256), jnp.float32)
        _lenS = 256 - jax.random.randint(jax.random.fold_in(_rk, 7), (8,), 0, max(1, 256 // 4) + 1, jnp.int32)
        _lenS2 = 77 - jax.random.randint(jax.random.fold_in(_rk, 8), (8,), 0, max(1, 77 // 4) + 1, jnp.int32)
        _ctx_1024P = jax.random.normal(jax.random.fold_in(_rk, 11), (8, 16, 256), jnp.float32)
        _ctx_1024c = jax.random.dirichlet(jax.random.fold_in(_rk, 511), 0.3 * jnp.ones((16,), jnp.float32), (8, 77))
        _ctx_1024t = jnp.einsum('bsk,bkd->bsd', _ctx_1024c, _ctx_1024P)
        _ctx_1024t = _ctx_1024t * jax.lax.rsqrt(jnp.mean(jnp.square(_ctx_1024t)) + 1e-12) * 0.953939
        ctx_1024 = -0.000292821 + 1.00034 * (_ctx_1024t + 0.3 * jax.random.normal(jax.random.fold_in(_rk, 611), (8, 77, 256), jnp.float32))
        _validS = jnp.arange(256)[None, :] < _lenS[:, None]
        _validS2 = jnp.arange(77)[None, :] < _lenS2[:, None]
        _causal = jnp.tril(jnp.ones((256, 256), dtype=bool))
        mask_Bx1x1xS2_if1 = jnp.where(jnp.ones((8, 1, 1, 77), dtype=bool), 1, 0).astype(jnp.int32)
        mask_BxSxS2_ik1 = jnp.where(jnp.broadcast_to(_validS2[:, None, :], (8, 256, 77)), 1, 0).astype(jnp.int32)
        return (x, ctx_1024, mask_Bx1x1xS2_if1, mask_BxSxS2_ik1)
    x, ctx_1024, mask_Bx1x1xS2_if1, mask_BxSxS2_ik1 = _rec_inputs()

    def _L0_xattn_setup():
        import jax, jax.numpy as jnp
        import numpy as np
        EMBED = 256
        HEADS = 16
        HEAD_DIM = EMBED // HEADS
        FF = 4 * EMBED
        EPS = 1e-05

        def layernorm(x, g, b):
            mu = jnp.mean(x, axis=-1, keepdims=True)
            var = jnp.mean((x - mu) ** 2, axis=-1, keepdims=True)
            return (x - mu) * jax.lax.rsqrt(var + EPS) * g + b
        key = jax.random.key(seed)
        ks = jax.random.split(key, 16)
        B, S = (2, 512)
        f32 = jnp.float32
        inp = {'value': jax.random.normal(ks[0], (B, S, EMBED), f32), 'key': jax.random.normal(ks[1], (B, S, EMBED), f32), 'query': jax.random.normal(ks[2], (B, S, EMBED), f32), 'mask': jnp.ones((B, 1, 1, S), jnp.int32), 'wv': jax.random.normal(ks[3], (HEAD_DIM, HEAD_DIM), f32) * 0.02, 'wk': jax.random.normal(ks[4], (HEAD_DIM, HEAD_DIM), f32) * 0.02, 'wq': jax.random.normal(ks[5], (HEAD_DIM, HEAD_DIM), f32) * 0.02, 'w_out': jax.random.normal(ks[6], (EMBED, EMBED), f32) * 0.02, 'b_out': jnp.zeros((EMBED,), f32), 'g1': jnp.ones((EMBED,), f32), 'beta1': jnp.zeros((EMBED,), f32), 'w_ff1': jax.random.normal(ks[7], (EMBED, FF), f32) * 0.02, 'b_ff1': jnp.zeros((FF,), f32), 'w_ff2': jax.random.normal(ks[8], (FF, EMBED), f32) * 0.02, 'b_ff2': jnp.zeros((EMBED,), f32), 'g2': jnp.ones((EMBED,), f32), 'beta2': jnp.zeros((EMBED,), f32)}
        return inp
    _L0_xattn_all = _L0_xattn_setup()
    _L0_xattn_in = {k: v for k, v in _L0_xattn_all.items() if k in ('wv', 'wk', 'wq', 'w_out', 'b_out', 'g1', 'beta1', 'w_ff1', 'b_ff1', 'w_ff2', 'b_ff2', 'g2', 'beta2')}
    del _L0_xattn_all

    def _L1_xattn_setup():
        import jax, jax.numpy as jnp
        import numpy as np
        D_MODEL = 256
        N_HEAD = 16
        D_K = D_MODEL // N_HEAD
        LN_EPS = 1e-05

        def _split_heads(x, W):
            B, S, _ = x.shape
            y = jnp.einsum('bsd,ed->bse', x, W)
            return y.reshape(B, S, N_HEAD, D_K).transpose(0, 2, 1, 3)
        key = jax.random.key(seed)
        ks = jax.random.split(key, 9)
        B, S = (4, 512)
        scale = 1.0 / np.sqrt(D_MODEL)
        return {'query': jax.random.normal(ks[0], (B, S, D_MODEL), jnp.float32), 'key': jax.random.normal(ks[1], (B, S, D_MODEL), jnp.float32), 'value': jax.random.normal(ks[2], (B, S, D_MODEL), jnp.float32), 'mask': jax.random.randint(ks[3], (B, S, S), 0, 2, jnp.int32), 'W_Q': jax.random.normal(ks[4], (D_MODEL, D_MODEL), jnp.float32) * scale, 'W_K': jax.random.normal(ks[5], (D_MODEL, D_MODEL), jnp.float32) * scale, 'W_V': jax.random.normal(ks[6], (D_MODEL, D_MODEL), jnp.float32) * scale, 'W_O': jax.random.normal(ks[7], (D_MODEL, D_MODEL), jnp.float32) * scale, 'gamma': jnp.ones((D_MODEL,), jnp.float32), 'beta': jnp.zeros((D_MODEL,), jnp.float32)}
    _L1_xattn_all = _L1_xattn_setup()
    _L1_xattn_in = {k: v for k, v in _L1_xattn_all.items() if k in ('W_Q', 'W_K', 'W_V', 'W_O', 'gamma', 'beta')}
    del _L1_xattn_all
    return {'x': x, 'ctx_1024': ctx_1024, 'mask_Bx1x1xS2_if1': mask_Bx1x1xS2_if1, 'mask_BxSxS2_ik1': mask_BxSxS2_ik1, 'L0_xattn_wv': _L0_xattn_in['wv'], 'L0_xattn_wk': _L0_xattn_in['wk'], 'L0_xattn_wq': _L0_xattn_in['wq'], 'L0_xattn_w_out': _L0_xattn_in['w_out'], 'L0_xattn_b_out': _L0_xattn_in['b_out'], 'L0_xattn_g1': _L0_xattn_in['g1'], 'L0_xattn_beta1': _L0_xattn_in['beta1'], 'L0_xattn_w_ff1': _L0_xattn_in['w_ff1'], 'L0_xattn_b_ff1': _L0_xattn_in['b_ff1'], 'L0_xattn_w_ff2': _L0_xattn_in['w_ff2'], 'L0_xattn_b_ff2': _L0_xattn_in['b_ff2'], 'L0_xattn_g2': _L0_xattn_in['g2'], 'L0_xattn_beta2': _L0_xattn_in['beta2'], 'L1_xattn_W_Q': _L1_xattn_in['W_Q'], 'L1_xattn_W_K': _L1_xattn_in['W_K'], 'L1_xattn_W_V': _L1_xattn_in['W_V'], 'L1_xattn_W_O': _L1_xattn_in['W_O'], 'L1_xattn_gamma': _L1_xattn_in['gamma'], 'L1_xattn_beta': _L1_xattn_in['beta']}

def reference(x, ctx_1024, mask_Bx1x1xS2_if1, mask_BxSxS2_ik1, L0_xattn_wv, L0_xattn_wk, L0_xattn_wq, L0_xattn_w_out, L0_xattn_b_out, L0_xattn_g1, L0_xattn_beta1, L0_xattn_w_ff1, L0_xattn_b_ff1, L0_xattn_w_ff2, L0_xattn_b_ff2, L0_xattn_g2, L0_xattn_beta2, L1_xattn_W_Q, L1_xattn_W_K, L1_xattn_W_V, L1_xattn_W_O, L1_xattn_gamma, L1_xattn_beta):
    import jax
    import jax.numpy as jnp

    def _L0_xattn_ref(value, key, query, mask, wv, wk, wq, w_out, b_out, g1, beta1, w_ff1, b_ff1, w_ff2, b_ff2, g2, beta2):
        import jax, jax.numpy as jnp
        import numpy as np
        EMBED = 256
        HEADS = 16
        HEAD_DIM = EMBED // HEADS
        FF = 4 * EMBED
        EPS = 1e-05

        def layernorm(x, g, b):
            mu = jnp.mean(x, axis=-1, keepdims=True)
            var = jnp.mean((x - mu) ** 2, axis=-1, keepdims=True)
            return (x - mu) * jax.lax.rsqrt(var + EPS) * g + b
        B, S, E = query.shape
        v = value.reshape(B, -1, HEADS, HEAD_DIM) @ wv
        k = key.reshape(B, -1, HEADS, HEAD_DIM) @ wk
        q = query.reshape(B, -1, HEADS, HEAD_DIM) @ wq
        scores = jnp.einsum('bqhd,bkhd->bhqk', q, k)
        scores = jnp.where(mask == 0, jnp.float32(-1e+20), scores)
        attn = jax.nn.softmax(scores / jnp.sqrt(jnp.float32(EMBED)), axis=-1)
        out = jnp.einsum('bhqk,bkhd->bqhd', attn, v).reshape(B, S, E)
        attention = out @ w_out + b_out
        x = layernorm(attention + query, g1, beta1)
        ff = jax.nn.relu(x @ w_ff1 + b_ff1) @ w_ff2 + b_ff2
        return layernorm(ff + x, g2, beta2)

    def _L1_xattn_ref(query, key, value, mask, W_Q, W_K, W_V, W_O, gamma, beta):
        import jax, jax.numpy as jnp
        import numpy as np
        D_MODEL = 256
        N_HEAD = 16
        D_K = D_MODEL // N_HEAD
        LN_EPS = 1e-05

        def _split_heads(x, W):
            B, S, _ = x.shape
            y = jnp.einsum('bsd,ed->bse', x, W)
            return y.reshape(B, S, N_HEAD, D_K).transpose(0, 2, 1, 3)
        residual = query
        B, S, _ = query.shape
        q = _split_heads(query, W_Q)
        k = _split_heads(key, W_K)
        v = _split_heads(value, W_V)
        scores = jnp.einsum('bhqd,bhkd->bhqk', q, k) / np.sqrt(D_K)
        scores = jnp.where(mask[:, None, :, :] == 1, jnp.float32(-1000000000.0), scores)
        p = jax.nn.softmax(scores, axis=-1)
        ctx = jnp.einsum('bhqk,bhkd->bhqd', p, v)
        concat = ctx.transpose(0, 2, 1, 3).reshape(B, S, D_MODEL)
        out = jnp.einsum('bsd,ed->bse', concat, W_O) + residual
        mu = jnp.mean(out, axis=-1, keepdims=True)
        var = jnp.mean((out - mu) ** 2, axis=-1, keepdims=True)
        return (out - mu) * jax.lax.rsqrt(var + LN_EPS) * gamma + beta
    x = _L0_xattn_ref(ctx_1024, ctx_1024, x, mask_Bx1x1xS2_if1, L0_xattn_wv, L0_xattn_wk, L0_xattn_wq, L0_xattn_w_out, L0_xattn_b_out, L0_xattn_g1, L0_xattn_beta1, L0_xattn_w_ff1, L0_xattn_b_ff1, L0_xattn_w_ff2, L0_xattn_b_ff2, L0_xattn_g2, L0_xattn_beta2)
    x = _L1_xattn_ref(x, ctx_1024, ctx_1024, mask_BxSxS2_ik1, L1_xattn_W_Q, L1_xattn_W_K, L1_xattn_W_V, L1_xattn_W_O, L1_xattn_gamma, L1_xattn_beta)
    return x

_drawn_inputs = setup_inputs


def setup_inputs(seed=0):
    import zlib

    import numpy as np

    out = dict(_drawn_inputs(seed))
    spreads = {'L0_xattn_b_out': (0.0, 0.1),
     'L0_xattn_g1': (1.0, 0.2),
     'L0_xattn_beta1': (0.0, 0.1),
     'L0_xattn_b_ff1': (0.0, 0.1),
     'L0_xattn_b_ff2': (0.0, 0.1),
     'L0_xattn_g2': (1.0, 0.2),
     'L0_xattn_beta2': (0.0, 0.1),
     'L1_xattn_gamma': (1.0, 0.2),
     'L1_xattn_beta': (0.0, 0.1)}
    factors = {'L0_xattn_wv': 5.503,
     'L0_xattn_wk': 26.439,
     'L0_xattn_wq': 27.878,
     'L0_xattn_w_out': 5.461}
    for name, (base, spread) in spreads.items():
        noise = np.random.default_rng([zlib.crc32(name.encode()), seed]).standard_normal(out[name].shape)
        drawn = base * np.exp(spread * noise) if base else spread * noise
        out[name] = jnp.asarray(drawn.astype(out[name].dtype))
    for name, factor in factors.items():
        out[name] = (out[name] * factor).astype(out[name].dtype)
    return out
```

```python
from contextlib import ExitStack

import concourse.bass as bass
from concourse import mybir

F32 = mybir.dt.float32
BF16 = mybir.dt.bfloat16
I32 = mybir.dt.int32
ALU = mybir.AluOpType
ACT = mybir.ActivationFunctionType
AX_X = mybir.AxisListType.X

P = 128
B = 8
S = 256
KEYS = 77
E = 256
FF = 1024
HEADS = 16
HD = E // HEADS
QT = S // P
EC = E // P
FC = FF // P
HH = HEADS // EC
UNITS = QT * EC
BH = 4
K_A = 64
K_B = 16
PAIRS = HH // 2
PW = 2 * HD + 2
TCOLS = HH * (K_A + K_B)
MASKED = -1.0e20
EPS = 1e-5
SCALE = (1.0 / float(E) ** 0.5, 1.0 / float(HD) ** 0.5)


def nth(batch, per, k=0):
    return batch * per + (k + 1)


def build(nc, d, out):
    ctx = ExitStack()
    with ctx:
        def sb(name, shape, dt=F32):
            return ctx.enter_context(nc.sbuf_tensor(name, shape, dt))

        def pb(name, shape, dt=F32):
            return ctx.enter_context(nc.psum_tensor(name, shape, dt))

        def sem(name):
            return ctx.enter_context(nc.semaphore(name))

        def pair(name):
            return [sem(f"{name}_l0"), sem(f"{name}_l1")]

        ident = sb("ident", [P, P])
        ident_b = sb("ident_b", [P, P], BF16)
        head_mask = sb("head_mask", [P, HH])
        v_mask = sb("v_mask", [P, 2, 2 * PAIRS, PW])
        cols = sb("cols", [P, 4 * EC + FC])
        rows = sb("rows", [P, 8, E])
        g1c, beta1c, g2c, beta2c = (cols[:, EC * n:EC * n + EC] for n in range(4))
        bff1c = cols[:, 4 * EC:]
        b_out_r, g1_r, beta1_r, b_ff2_r, g2_r, beta2_r, gamma_r, beta_r = (rows[:, n, :] for n in range(8))
        beta1_ff2_r = sb("beta1_ff2_r", [P, E])
        wk_rep = sb("wk_rep", [HD, P])
        wq_rep = sb("wq_rep", [HD, P])
        wv_rep = sb("wv_rep", [P, P])
        wv_bd = sb("wv_bd", [P, P])
        g_bd = sb("g_bd", [P, P])
        w_out = sb("w_out", [P, EC, E])
        w_vout = sb("w_vout", [P, EC, E])
        w1 = sb("w1", [P, EC, FF])
        w2 = sb("w2", [P, FC, E])
        wq1 = sb("wq1", [P, EC, E])
        wk1 = sb("wk1", [P, EC, E])
        wv1 = sb("wv1", [P, EC, E])
        wo1 = sb("wo1", [P, EC, E])
        neg_half = sb("neg_half", [P, QT])
        eps = sb("eps", [P, QT])

        x_t = sb("x_t", [P, EC, S])
        x_n = sb("x_n", [P, QT, E])
        ctx_t = [sb(f"ctx_t{n}", [P, EC, 2 * P]) for n in range(2)]
        ctx_ab = sb("ctx_ab", [P, 2, E])
        m_i = [sb("m_i0", [P, 1, KEYS], I32), sb("m_i1", [P, QT, KEYS], I32)]
        m_bias = [sb("m_bias0", [P, 1, KEYS], BF16), sb("m_bias1", [P, QT, KEYS], BF16)]
        k_s = [sb(f"k_s{n}", [P, EC, KEYS]) for n in range(2)]
        k_bd = [sb(f"k_bd{n}", [P, EC, HH, KEYS]) for n in range(2)]
        v_bd = [sb(f"v_bd{n}", [P, 2, 2 * PAIRS, PW]) for n in range(2)]
        neg_max = sb("neg_max", [P, HH])
        diff = sb("diff", [P, HH, KEYS])
        prob = sb("prob", [P, TCOLS])
        prob_t = sb("prob_t", [P, TCOLS])
        rden = sb("rden", [P, 2 * PAIRS, 2])
        att = [sb(f"att{n}", [P, QT, E]) for n in range(2)]
        att_t = [sb(f"att_t{n}", [P, EC, S]) for n in range(2)]
        ysum = [sb(f"ysum{n}", [P, QT, E]) for n in range(3)]
        stats = [sb(f"stats{n}", [P, QT, 6]) for n in range(3)]
        mean_var = [sb(f"mean_var{n}", [P, QT, 2]) for n in range(3)]
        var_eps = [sb(f"var_eps{n}", [P, QT]) for n in range(3)]
        rstd = [sb(f"rstd{n}", [P, QT]) for n in range(3)]
        xhat = [sb(f"xhat{n}", [P, QT, E]) for n in range(3)]
        x1_t = sb("x1_t", [P, EC, S])
        x1_res = sb("x1_res", [P, QT, E])
        h_t = sb("h_t", [P, FC, S])
        x2_t = sb("x2_t", [P, EC, S])
        x2_res = sb("x2_res", [P, QT, E])
        q_t = sb("q_t", [P, EC, S])
        o_n = sb("o_n", [P, QT, E])

        p_s = pb("p_s", [P, 2, 512])
        p_t = pb("p_t", [P, 2, 512])
        p_v = pb("p_v", [P, 512])
        ring = [pb(f"ring{n}", [P, 512]) for n in range(3)]
        pt_flat = p_t[:, :, :].rearrange("p a b -> p (a b)")[:, 0:TCOLS]
        pv_all = p_v[:, 0:2 * PAIRS * PW].rearrange("p (j c) -> p j c", c=PW)

        ld_const = sem("ld_const")
        ld_l0w = sem("ld_l0w")
        ld_rows = sem("ld_rows")
        ld_kv1w = sem("ld_kv1w")
        ld_ffw = sem("ld_ffw")
        ld_qo1w = sem("ld_qo1w")
        ld_xt = sem("ld_xt")
        ld_xn = sem("ld_xn")
        ld_ctx_t = pair("ld_ctx_t")
        ld_ctx_ab = sem("ld_ctx_ab")
        ld_mask = pair("ld_mask")
        stored = sem("stored")
        ident_b_ready = sem("ident_b_ready")
        pad_ready = sem("pad_ready")
        half_ready = sem("half_ready")
        ones_ready = sem("ones_ready")
        g_mm = sem("g_mm")
        g_ready = sem("g_ready")
        wv_bd_ready = sem("wv_bd_ready")
        wvout_mm = sem("wvout_mm")
        wvout_ready = sem("wvout_ready")
        beta1_ff2_ready = sem("beta1_ff2_ready")
        k_mm = pair("k_mm")
        k_copied = pair("k_copied")
        k_bd_ready = pair("k_bd_ready")
        v1_mm = sem("v1_mm")
        v_bd_ready = pair("v_bd_ready")
        bias_ready = pair("bias_ready")
        scores_mm = pair("scores_mm")
        max_ready = pair("max_ready")
        diff_ready = pair("diff_ready")
        prob_ready = pair("prob_ready")
        turned_mm = pair("turned_mm")
        prob_t_ready = pair("prob_t_ready")
        pv_mm = pair("pv_mm")
        rden_ready = pair("rden_ready")
        att_ready = pair("att_ready")
        att_t_mm = pair("att_t_mm")
        att_t_ready = pair("att_t_ready")
        proj_mm = pair("proj_mm")
        xres_ready = sem("xres_ready")
        y_ready = [sem(f"y_ready{n}") for n in range(3)]
        stats_ready = [sem(f"stats_ready{n}") for n in range(3)]
        mv_ready = [sem(f"mv_ready{n}") for n in range(3)]
        rstd_ready = [sem(f"rstd_ready{n}") for n in range(3)]
        xhat_ready = [sem(f"xhat_ready{n}") for n in range(3)]
        x_t_mm = pair("x_t_mm")
        x_t_ready = pair("x_t_ready")
        x1_res_ready = sem("x1_res_ready")
        x2_res_ready = sem("x2_res_ready")
        h_mm = sem("h_mm")
        h_ready = sem("h_ready")
        ff2_mm = sem("ff2_mm")
        q_mm = sem("q_mm")
        q_ready = sem("q_ready")
        o_ready = sem("o_ready")

        block = ctx.enter_context(nc.Block())

        def iterations(eng, body):
            body(0, 0, None, None)
            body(1, 1, 0, None)
            with eng.Fori(2, B - 1) as i:
                body(i, i, i - 1, i - 2)
            body(B - 1, B - 1, B - 2, B - 3)
            body(B, None, B - 1, B - 2)
            body(B + 1, None, None, B - 1)

        def more(b):
            return b is not None and not (isinstance(b, int) and b + 1 >= B)

        def later(b):
            return not (isinstance(b, int) and b == 0)

        @block.sync
        def _(sp):
            def of_batch(a, b):
                return a[bass.ds(b * P, P)] if not isinstance(b, int) else a[b * P:b * P + P]

            def load_ctx_t(layer, b):
                sp.dma_start(ctx_t[layer][:], of_batch(d["ctx_t"], b)).then_inc(ld_ctx_t[layer], 16)

            def load_mask(layer, b):
                sp.dma_start(m_i[layer][:], of_batch(d["mask0" if layer == 0 else "mask1"], b)).then_inc(ld_mask[layer], 16)

            load_ctx_t(0, 0)
            sp.dma_start(wk_rep[:], d["wk_rep"]).then_inc(ld_l0w, 16)
            sp.dma_start(wq_rep[:], d["wq_rep"]).then_inc(ld_l0w, 16)
            sp.dma_start(head_mask[:], d["head_mask"]).then_inc(ld_l0w, 16)
            sp.dma_start(ident[:], d["ident"]).then_inc(ld_const, 16)
            sp.dma_start(x_t[:], of_batch(d["x_t"], 0)).then_inc(ld_xt, 16)
            load_mask(0, 0)
            sp.dma_start(v_mask[:], d["v_mask"]).then_inc(ld_const, 16)
            sp.dma_start(ctx_ab[:], of_batch(d["ctx_ab"], 0)).then_inc(ld_ctx_ab, 16)
            sp.dma_start(wv_rep[:], d["wv_rep"]).then_inc(ld_l0w, 16)
            sp.dma_start(w_out[:], d["w_out"]).then_inc(ld_l0w, 16)
            sp.dma_start(rows[:], d["rows"]).then_inc(ld_rows, 16)
            sp.dma_start(cols[:], d["cols"]).then_inc(ld_rows, 16)
            sp.dma_start(x_n[:], of_batch(d["x_n"], 0)).then_inc(ld_xn, 16)
            sp.dma_start(w1[:], d["w1"]).then_inc(ld_ffw, 16)
            sp.dma_start(wk1[:], d["wk1"]).then_inc(ld_kv1w, 16)
            sp.dma_start(wv1[:], d["wv1"]).then_inc(ld_kv1w, 16)
            sp.dma_start(w2[:], d["w2"]).then_inc(ld_ffw, 16)
            sp.dma_start(wq1[:], d["wq1"]).then_inc(ld_qo1w, 16)
            sp.dma_start(wo1[:], d["wo1"]).then_inc(ld_qo1w, 16)

            def body(i, b, p, t):
                if more(b):
                    sp.wait_ge(k_mm[0], nth(b, 1))
                    load_ctx_t(0, b + 1)
                    sp.wait_ge(bias_ready[0], nth(b, 1))
                    load_mask(0, b + 1)
                    sp.wait_ge(v_bd_ready[0], nth(b, 1))
                    sp.dma_start(ctx_ab[:], of_batch(d["ctx_ab"], b + 1)).then_inc(ld_ctx_ab, 16)
                if b is not None:
                    if p is not None:
                        sp.wait_ge(k_mm[1], nth(p, 1))
                        sp.wait_ge(v1_mm, nth(p, 1))
                    load_ctx_t(1, b)
                    if p is not None:
                        sp.wait_ge(bias_ready[1], nth(p, 1))
                    load_mask(1, b)
                if more(b):
                    sp.wait_ge(scores_mm[0], nth(b, UNITS, UNITS - 1))
                    sp.dma_start(x_t[:], of_batch(d["x_t"], b + 1)).then_inc(ld_xt, 16)
                if t is not None:
                    sp.wait_ge(o_ready, nth(t, 2, 1))
                    sp.dma_start(of_batch(out, t), o_n[:]).then_inc(stored, 16)
                if more(b):
                    sp.wait_ge(y_ready[0], nth(b, 1))
                    sp.dma_start(x_n[:], of_batch(d["x_n"], b + 1)).then_inc(ld_xn, 16)

            iterations(sp, body)
            sp.wait_ge(stored, 16 * B)

        @block.tensor
        def _(pe):
            q_of = [x_t, q_t]

            def scores(layer, b, u, before):
                qt, half = u // EC, u % EC
                if u == 0:
                    if layer == 0:
                        pe.wait_ge(ld_xt, 16 * b + 16)
                    else:
                        pe.wait_ge(q_ready, nth(b, 1))
                    pe.wait_ge(bias_ready[layer], nth(b, 1))
                    pe.wait_ge(k_bd_ready[layer], nth(b, EC, EC - 1))
                if before is not None:
                    pe.wait_ge(diff_ready[before[0]], nth(before[1], UNITS, before[2]))
                for n in range(2):
                    o = p_s[:, n, 0:BH * KEYS]
                    bias = m_bias[layer][:, qt if layer else 0, :].unsqueeze(1).to_broadcast((P, BH, KEYS))
                    pe.matmul(o, ident_b[:], bias, start=True, stop=False)
                    last = pe.matmul(o, q_of[layer][:, half, qt * P:(qt + 1) * P],
                                     k_bd[layer][:, half, n * BH:(n + 1) * BH, :], start=False, stop=True)
                last.then_inc(scores_mm[layer], 1)

            def turn(layer, b, u, before):
                pe.wait_ge(prob_ready[layer], nth(b, UNITS, u))
                if before is not None:
                    pe.wait_ge(prob_t_ready[before[0]], nth(before[1], UNITS, before[2]))
                for j in range(PAIRS):
                    pe.transpose(p_t[:, 0, j * P:(j + 1) * P], prob[:, j * P:(j + 1) * P], ident[:])
                pe.transpose(p_t[:, 1, 0:P], prob[:, PAIRS * P:], ident[:]).then_inc(turned_mm[layer], 1)

            def values(layer, b, u, before):
                half = u % EC
                pe.wait_ge(prob_t_ready[layer], nth(b, UNITS, u))
                if u == 0:
                    pe.wait_ge(v_bd_ready[layer], nth(b, 1))
                if half == 0 and before is not None:
                    pe.wait_ge(att_ready[before[0]], nth(before[1], QT, before[2] // EC))
                for j in range(PAIRS):
                    pe.matmul(pv_all[:, half * PAIRS + j, :], prob_t[:, j * P:(j + 1) * P],
                              v_bd[layer][:, 0, half * PAIRS + j, :], start=(half == 0 and j == 0), stop=False,
                              skip_group_check=True)
                pe.matmul(pv_all[:, half * PAIRS:(half + 1) * PAIRS, :], prob_t[:, PAIRS * P:],
                          v_bd[layer][:, 1, half * PAIRS:(half + 1) * PAIRS, :], start=False, stop=True,
                          skip_group_check=True).then_inc(pv_mm[layer], 1)

            def keys(layer, b, bank):
                pe.wait_ge(ld_ctx_t[layer], 16 * b + 16)
                c_t = ctx_t[layer][:, :, K_A:K_A + KEYS]
                for m in range(EC):
                    o = bank[:, m * KEYS:(m + 1) * KEYS]
                    if layer == 0:
                        last = pe.matmul(o, g_bd[:], c_t[:, m, :], start=True, stop=True)
                    else:
                        for c in range(EC):
                            last = pe.matmul(o, wk1[:, c, m * P:(m + 1) * P], c_t[:, c, :],
                                             start=(c == 0), stop=(c == EC - 1))
                last.then_inc(k_mm[layer], 1)

            def values_1(b, bank):
                pe.wait_ge(ld_ctx_t[1], 16 * b + 16)
                for part in range(2):
                    for c in range(EC):
                        last = pe.matmul(bank[:, part * E:(part + 1) * E], ctx_t[1][:, c, part * P:(part + 1) * P], wv1[:, c, :],
                                         start=(c == 0), stop=(c == EC - 1))
                last.then_inc(v1_mm, 1)

            def turn_rows(src, bank):
                for c in range(EC):
                    for qt in range(QT):
                        last = pe.transpose(bank[:, c * S + qt * P:c * S + (qt + 1) * P],
                                            src[:, qt, c * P:(c + 1) * P], ident[:])
                return last

            def to_rows(lhs, w, chunks, bank, qt):
                for c in range(chunks):
                    last = pe.matmul(bank[:, qt * E:(qt + 1) * E], lhs[:, c, qt * P:(qt + 1) * P], w[:, c, :],
                                     start=(c == 0), stop=(c == chunks - 1))
                return last

            def attention_out(layer, b, bank):
                pe.wait_ge(att_ready[layer], nth(b, QT, QT - 1))
                turn_rows(att[layer], bank).then_inc(att_t_mm[layer], 1)

            def project(layer, b, bank):
                pe.wait_ge(att_t_ready[layer], nth(b, 1))
                for qt in range(QT):
                    last = to_rows(att_t[layer], (w_vout, wo1)[layer], EC, bank, qt)
                last.then_inc(proj_mm[layer], 1)

            def normed_to_columns(n, b, bank):
                pe.wait_ge(xhat_ready[n], nth(b, QT, QT - 1))
                turn_rows(xhat[n], bank).then_inc(x_t_mm[n], 1)

            def ff1(b, g, bank):
                if g == 0:
                    pe.wait_ge(x_t_ready[0], nth(b, 1))
                for f in (2 * g, 2 * g + 1):
                    for c in range(EC):
                        last = pe.matmul(bank[:, (f % 2) * S:(f % 2 + 1) * S], w1[:, c, f * P:(f + 1) * P], x1_t[:, c, :],
                                         start=(c == 0), stop=(c == EC - 1))
                last.then_inc(h_mm, 1)

            def query_1(b, bank):
                pe.wait_ge(x_t_ready[1], nth(b, 1))
                for m in range(EC):
                    for c in range(EC):
                        last = pe.matmul(bank[:, m * S:(m + 1) * S], wq1[:, c, m * P:(m + 1) * P], x2_t[:, c, :],
                                         start=(c == 0), stop=(c == EC - 1))
                last.then_inc(q_mm, 1)

            pe.wait_ge(ld_l0w, 16 * 5)
            pe.matmul(ring[0][:, 0:P], wk_rep[:], wq_rep[:], start=True, stop=True).then_inc(g_mm, 1)
            pe.wait_ge(wv_bd_ready, 1)
            for c in range(EC):
                last = pe.matmul(ring[2][:, c * E:(c + 1) * E], wv_bd[:], w_out[:, c, :], start=True, stop=True)
            last.then_inc(wvout_mm, 1)
            pe.wait_ge(g_ready, 1)
            keys(0, 0, ring[1])
            pe.wait_ge(ident_b_ready, 1)
            pe.wait_ge(ld_const, 32)

            def body(i, b, p, t):
                here = [(0, b, u) if b is not None else None for u in range(UNITS)]
                here += [(1, p, u) if p is not None else None for u in range(UNITS)]
                order = [(1, t, UNITS - 1) if t is not None else None] + here
                ahead = (1, t, UNITS - 2) if t is not None else None
                if t is None and p is not None:
                    order[0] = (0, p, UNITS - 1)

                for s in range(2 * UNITS):
                    unit, prev = order[s + 1], order[s]
                    prev2 = order[s - 1] if s else ahead
                    turn_prev = prev if not (s == 0 and t is None) else None
                    if unit is not None:
                        scores(*unit, prev)
                    if turn_prev is not None:
                        turn(*turn_prev, prev2)

                    if s == 0:
                        if p is not None:
                            if not later(p):
                                pe.wait_ge(ld_kv1w, 32)
                            pe.wait_ge(x_t_ready[0], nth(p, 1))
                            keys(1, p, ring[0])
                            for g in (2, 3):
                                pe.wait_ge(h_ready, nth(p, FC, 2 * g - 3))
                                ff1(p, g, ring[g - 1])
                    if s == 1 and p is not None:
                        pe.wait_ge(k_copied[1], nth(p, 1))
                        values_1(p, ring[0])
                        if not later(p):
                            pe.wait_ge(ld_ffw, 32)
                        pe.wait_ge(h_ready, nth(p, FC, FC - 1))
                        to_rows(h_t, w2, FC, ring[1], 0)
                    if s == 2 and p is not None:
                        to_rows(h_t, w2, FC, ring[1], 1).then_inc(ff2_mm, 1)
                    if s == 3:
                        if p is not None:
                            normed_to_columns(1, p, ring[2])
                        if t is not None:
                            if p is not None:
                                pe.wait_ge(v_bd_ready[1], nth(p, 1))
                            attention_out(1, t, ring[0])
                        if p is not None:
                            if not later(p):
                                pe.wait_ge(ld_qo1w, 32)
                            pe.wait_ge(y_ready[1], nth(p, 1))
                            query_1(p, ring[1])
                    if s == 4 and t is not None:
                        if p is not None:
                            pe.wait_ge(x_t_ready[1], nth(p, 1))
                        project(1, t, ring[2])
                    if s == 5 and b is not None:
                        if t is not None:
                            pe.wait_ge(att_t_ready[1], nth(t, 1))
                        attention_out(0, b, ring[0])
                        if more(b):
                            if p is not None:
                                pe.wait_ge(q_ready, nth(p, 1))
                            keys(0, b + 1, ring[1])
                        if not later(b):
                            pe.wait_ge(wvout_ready, 1)
                        if t is not None:
                            pe.wait_ge(y_ready[2], nth(t, 1))
                        project(0, b, ring[2])
                    if s == 6 and b is not None:
                        normed_to_columns(0, b, ring[0])
                    if s == 7 and b is not None:
                        if not later(b):
                            pe.wait_ge(ld_ffw, 32)
                        if more(b):
                            pe.wait_ge(k_copied[0], nth(b + 1, 1))
                        ff1(b, 0, ring[1])
                        pe.wait_ge(y_ready[0], nth(b, 1))
                        ff1(b, 1, ring[2])

                    if turn_prev is not None:
                        if s == 0:
                            tile_before = None
                        elif s == 1:
                            tile_before = order[0]
                        else:
                            tile_before = order[s - 1] if s % 2 else None
                        values(*turn_prev, tile_before)

            iterations(pe, body)

        @block.vector
        def _(dve):
            def bias_of(layer, b):
                dve.wait_ge(ld_mask[layer], 16 * b + 16)
                dve.tensor_scalar(m_bias[layer][:], m_i[layer][:], float(layer), MASKED, ALU.is_equal, ALU.mult)\
                   .then_inc(bias_ready[layer], 1)

            dve.memset(prob[:, HH * K_A:], 0.0).then_inc(pad_ready, 1)
            dve.wait_ge(ld_l0w, 16 * 5)
            by_head = head_mask[:].unsqueeze(2).to_broadcast((P, HH, HD))
            dve.tensor_tensor(wv_bd[:].rearrange("p (h c) -> p h c", h=HH), wv_rep[:].rearrange("p (h c) -> p h c", h=HH),
                              by_head, ALU.mult).then_inc(wv_bd_ready, 1)
            dve.wait_ge(g_mm, 1)
            dve.tensor_tensor(g_bd[:].rearrange("p (h c) -> p h c", h=HH), ring[0][:, 0:P].rearrange("p (h c) -> p h c", h=HH),
                              by_head, ALU.mult).then_inc(g_ready, 1)
            dve.wait_ge(ld_const, 32)
            dve.tensor_copy(ident_b[:], ident[:]).then_inc(ident_b_ready, 1)
            bias_of(0, 0)
            for layer in range(2):
                dve.tensor_copy(v_bd[layer][:, :, :, 2 * HD:], v_mask[:, :, :, 2 * HD:]).then_inc(ones_ready, 1)
            dve.wait_ge(ones_ready, 2)
            dve.wait_ge(wvout_mm, 1)
            dve.tensor_copy(w_vout[:].rearrange("p c e -> p (c e)"), ring[2][:]).then_inc(wvout_ready, 1)

            def shifted(layer, b, u, before):
                dve.wait_ge(scores_mm[layer], nth(b, UNITS, u))
                four = p_s[:, :, 0:BH * KEYS].rearrange("p n (h k) -> p n h k", h=BH)
                dve.tensor_reduce(neg_max[:].rearrange("p (n h) -> p n h", n=2), four, AX_X, ALU.max,
                                  negate=True).then_inc(max_ready[layer], 1)
                dve.wait_ge(max_ready[layer], nth(b, UNITS, u))
                if before is not None:
                    dve.wait_ge(prob_ready[before[0]], nth(before[1], UNITS, before[2]))
                dve.tensor_tensor(diff[:].rearrange("p (n h) k -> p n h k", n=2), four,
                                  neg_max[:].rearrange("p (n h) -> p n h", n=2).unsqueeze(3).to_broadcast((P, 2, BH, KEYS)),
                                  ALU.add).then_inc(diff_ready[layer], 1)

            def normalise(layer, b, qt):
                dve.wait_ge(pv_mm[layer], nth(b, UNITS, qt * EC + EC - 1))
                dve.reciprocal(rden[:], pv_all[:, :, 2 * HD:]).then_inc(rden_ready[layer], 1)
                dve.wait_ge(rden_ready[layer], nth(b, QT, qt))
                dve.tensor_tensor(att[layer][:, qt, :].rearrange("p (j h c) -> p j h c", h=2, c=HD),
                                  pv_all[:, :, 0:2 * HD].rearrange("p j (h c) -> p j h c", h=2),
                                  rden[:].unsqueeze(3).to_broadcast((P, 2 * PAIRS, 2, HD)), ALU.mult)\
                   .then_inc(att_ready[layer], 1)

            def sum_and_stats(n, b, bank, res):
                dve.tensor_tensor(ysum[n][:].rearrange("p q e -> p (q e)"), bank[:], res[:].rearrange("p q e -> p (q e)"),
                                  ALU.add).then_inc(y_ready[n], 1)
                dve.wait_ge(y_ready[n], nth(b, 1))
                for qt in range(QT):
                    dve.bn_stats(stats[n][:, qt, :], ysum[n][:, qt, :]).then_inc(stats_ready[n], 1)
                dve.drain()
                for qt in range(QT):
                    dve.bn_aggr(mean_var[n][:, qt, :], stats[n][:, qt, :]).then_inc(mv_ready[n], 1)

            def normed(n, b):
                dve.wait_ge(rstd_ready[n], nth(b, 2, 1))
                for qt in range(QT):
                    dve.tensor_scalar(xhat[n][:, qt, :], ysum[n][:, qt, :], mean_var[n][:, qt, 0:1],
                                      rstd[n][:, qt:qt + 1], ALU.subtract, ALU.mult).then_inc(xhat_ready[n], 1)

            def body(i, b, p, t):
                here = [(0, b, u) if b is not None else None for u in range(UNITS)]
                here += [(1, p, u) if p is not None else None for u in range(UNITS)]
                ahead = (1, t, UNITS - 1) if t is not None else (0, p, UNITS - 1) if p is not None else None
                for s in range(2 * UNITS):
                    if s == 2 and p is not None:
                        if later(p):
                            dve.wait_ge(scores_mm[1], nth(p - 1, UNITS, UNITS - 1))
                        bias_of(1, p)
                    if s == 5 and more(b):
                        dve.wait_ge(scores_mm[0], nth(b, UNITS, UNITS - 1))
                        bias_of(0, b + 1)
                    if s == 1 and t is not None:
                        normalise(1, t, 1)
                    if s == 3 and b is not None:
                        normalise(0, b, 0)
                    if s == 3 and p is not None:
                        dve.wait_ge(ff2_mm, nth(p, 1))
                        dve.wait_ge(x1_res_ready, nth(p, 2, 1))
                        sum_and_stats(1, p, ring[1], x1_res)
                    if s == 5 and b is not None:
                        normalise(0, b, 1)
                    if s == 5 and t is not None:
                        dve.wait_ge(proj_mm[1], nth(t, 1))
                        dve.wait_ge(x2_res_ready, nth(t, 2, 1))
                        sum_and_stats(2, t, ring[2], x2_res)
                    if s == 6 and b is not None:
                        dve.wait_ge(proj_mm[0], nth(b, 1))
                        dve.wait_ge(xres_ready, nth(b, 1))
                        sum_and_stats(0, b, ring[2], x_n)
                    if s == 7 and p is not None:
                        normalise(1, p, 0)
                    unit = here[s]
                    before = here[s - 1] if s else ahead
                    if unit is not None:
                        shifted(*unit, before)
                    if s == 1 and p is not None:
                        dve.wait_ge(v1_mm, nth(p, 1))
                        dve.tensor_tensor(v_bd[1][:, :, :, 0:2 * HD], ring[0][:].rearrange("p (a j c) -> p a j c", a=2, c=2 * HD),
                                          v_mask[:, :, :, 0:2 * HD], ALU.mult).then_inc(v_bd_ready[1], 1)
                    if s == 3 and p is not None:
                        if later(p):
                            dve.wait_ge(x2_res_ready, nth(p - 1, 2, 1))
                        normed(1, p)
                    if s == 5 and t is not None:
                        if later(t):
                            dve.wait_ge(o_ready, nth(t - 1, 2, 1))
                        normed(2, t)
                    if s == 6 and b is not None:
                        normed(0, b)

            iterations(dve, body)

        @block.scalar
        def _(act):
            def exponential(layer, b, u, before):
                act.wait_ge(diff_ready[layer], nth(b, UNITS, u))
                if before is not None:
                    act.wait_ge(turned_mm[before[0]], nth(before[1], UNITS, before[2]))
                act.activation(prob[:, 0:HH * K_A].rearrange("p (h k) -> p h k", h=HH), diff[:, :, 0:K_A], ACT.Exp,
                               scale=SCALE[layer])
                act.activation(prob[:, HH * K_A:].rearrange("p (h k) -> p h k", h=HH)[:, :, 0:KEYS - K_A],
                               diff[:, :, K_A:], ACT.Exp, scale=SCALE[layer]).then_inc(prob_ready[layer], 1)

            def copy_turned(layer, b, u, before):
                act.wait_ge(turned_mm[layer], nth(b, UNITS, u))
                if before is not None:
                    act.wait_ge(pv_mm[before[0]], nth(before[1], UNITS, before[2]))
                act.activation(prob_t[:], pt_flat, ACT.Copy).then_inc(prob_t_ready[layer], 1)

            def copy_keys(layer, b, bank):
                act.wait_ge(k_mm[layer], nth(b, 1))
                act.activation(k_s[layer][:].rearrange("p c k -> p (c k)"), bank[:, 0:EC * KEYS], ACT.Copy)\
                   .then_inc(k_copied[layer], 1)

            def copy_att(layer, b, bank):
                act.wait_ge(att_t_mm[layer], nth(b, 1))
                act.activation(att_t[layer][:].rearrange("p c q -> p (c q)"), bank[:], ACT.Copy)\
                   .then_inc(att_t_ready[layer], 1)

            def scaled(n, b, bank, dst, g, beta):
                act.wait_ge(x_t_mm[n], nth(b, 1))
                for c in range(EC):
                    last = act.activation(dst[:, c, :], bank[:, c * S:(c + 1) * S], ACT.Identity,
                                          bias=beta[:, c:c + 1], scale=g[:, c:c + 1])
                last.then_inc(x_t_ready[n], 1)

            def hidden(b, g, bank):
                act.wait_ge(h_mm, nth(b, FC // 2, g))
                for f in (2 * g, 2 * g + 1):
                    act.activation(h_t[:, f, :], bank[:, (f % 2) * S:(f % 2 + 1) * S], ACT.Relu,
                                   bias=bff1c[:, f:f + 1]).then_inc(h_ready, 1)

            copy_keys(0, 0, ring[1])
            act.wait_ge(ld_rows, 32)
            act.wait_ge(pad_ready, 1)

            def body(i, b, p, t):
                here = [(0, b, u) if b is not None else None for u in range(UNITS)]
                here += [(1, p, u) if p is not None else None for u in range(UNITS)]
                ahead = (1, t, UNITS - 1) if t is not None else (0, p, UNITS - 1) if p is not None else None
                for s in range(2 * UNITS):
                    unit = here[s]
                    prev = here[s - 1] if s else ahead
                    prev2 = here[s - 2] if s > 1 else ahead if s else (1, t, UNITS - 2) if t is not None else None
                    if prev is not None and not (s == 0 and t is None):
                        copy_turned(*prev, prev2)
                    if unit is not None:
                        exponential(*unit, prev)
                    if s == 0 and p is not None:
                        copy_keys(1, p, ring[0])
                        hidden(p, 2, ring[1])
                        hidden(p, 3, ring[2])
                    if s == 3:
                        if p is not None:
                            scaled(1, p, ring[2], x2_t, g2c, beta2c)
                        if t is not None:
                            copy_att(1, t, ring[0])
                        if p is not None:
                            act.wait_ge(q_mm, nth(p, 1))
                            act.activation(q_t[:].rearrange("p c q -> p (c q)"), ring[1][:], ACT.Copy).then_inc(q_ready, 1)
                    if s == 5 and b is not None:
                        copy_att(0, b, ring[0])
                        if more(b):
                            copy_keys(0, b + 1, ring[1])
                    if s == 6 and b is not None:
                        scaled(0, b, ring[0], x1_t, g1c, beta1c)
                    if s == 7 and b is not None:
                        hidden(b, 0, ring[1])
                        hidden(b, 1, ring[2])

            iterations(act, body)

        @block.gpsimd
        def _(pool):
            def block_keys(layer, b):
                pool.wait_ge(k_copied[layer], nth(b, 1))
                for c in range(EC):
                    pool.tensor_tensor(k_bd[layer][:, c, :, :],
                                       k_s[layer][:, c, :].unsqueeze(1).to_broadcast((P, HH, KEYS)),
                                       head_mask[:].unsqueeze(2).to_broadcast((P, HH, KEYS)), ALU.mult)\
                        .then_inc(k_bd_ready[layer], 1)

            def block_values_0(b):
                pool.wait_ge(ld_ctx_ab, 16 * b + 16)
                pool.tensor_tensor(v_bd[0][:, :, :, 0:2 * HD], ctx_ab[:].rearrange("p a (j c) -> p a j c", c=2 * HD),
                                   v_mask[:, :, :, 0:2 * HD], ALU.mult).then_inc(v_bd_ready[0], 1)

            def inverse_deviation(n, b):
                pool.wait_ge(mv_ready[n], nth(b, QT, QT - 1))
                pool.tensor_tensor(var_eps[n][:], mean_var[n][:, :, 1], eps[:], ALU.add).then_inc(rstd_ready[n], 1)
                pool.wait_ge(rstd_ready[n], nth(b, 2, 0))
                pool.tensor_tensor(rstd[n][:], var_eps[n][:], neg_half[:], ALU.pow).then_inc(rstd_ready[n], 1)

            def gain_and_shift(n, b, dst, g, shift, done):
                pool.wait_ge(xhat_ready[n], nth(b, QT, QT - 1))
                wide = (P, QT, E)
                pool.tensor_tensor(dst[:], xhat[n][:], g.unsqueeze(1).to_broadcast(wide), ALU.mult).then_inc(done, 1)
                pool.wait_ge(done, nth(b, 2, 0))
                pool.tensor_tensor(dst[:], dst[:], shift.unsqueeze(1).to_broadcast(wide), ALU.add).then_inc(done, 1)

            pool.memset(neg_half[:], -0.5).then_inc(half_ready, 1)
            pool.memset(eps[:], EPS).then_inc(half_ready, 1)
            pool.wait_ge(half_ready, 2)
            pool.wait_ge(ld_l0w, 16 * 5)
            block_keys(0, 0)
            pool.wait_ge(ld_const, 32)
            pool.wait_ge(ones_ready, 2)
            block_values_0(0)
            pool.wait_ge(ld_rows, 32)
            pool.tensor_tensor(beta1_ff2_r[:], beta1_r, b_ff2_r, ALU.add).then_inc(beta1_ff2_ready, 1)
            pool.wait_ge(beta1_ff2_ready, 1)

            def body(i, b, p, t):
                if b is not None:
                    pool.wait_ge(ld_xn, 16 * b + 16)
                    pool.tensor_tensor(x_n[:], x_n[:], b_out_r.unsqueeze(1).to_broadcast((P, QT, E)), ALU.add)\
                        .then_inc(xres_ready, 1)
                if p is not None:
                    if later(p):
                        pool.wait_ge(scores_mm[1], nth(p - 1, UNITS, UNITS - 1))
                    block_keys(1, p)
                    inverse_deviation(1, p)
                if more(b):
                    pool.wait_ge(pv_mm[0], nth(b, UNITS, UNITS - 1))
                    block_values_0(b + 1)
                if t is not None:
                    inverse_deviation(2, t)
                if p is not None:
                    if later(p):
                        pool.wait_ge(y_ready[2], nth(p - 1, 1))
                    gain_and_shift(1, p, x2_res, g2_r, beta2_r, x2_res_ready)
                if b is not None:
                    inverse_deviation(0, b)
                if more(b):
                    block_keys(0, b + 1)
                if t is not None:
                    if later(t):
                        pool.wait_ge(stored, 16 * t)
                    gain_and_shift(2, t, o_n, gamma_r, beta_r, o_ready)
                if b is not None:
                    if p is not None:
                        pool.wait_ge(y_ready[1], nth(p, 1))
                    gain_and_shift(0, b, x1_res, g1_r, beta1_ff2_r[:], x1_res_ready)

            iterations(pool, body)


def kernel(**inputs):
    import numpy as np
    import concourse.bacc as bacc
    from concourse import mybir as mb
    from concourse.bass_utils import run_bass_kernel_spmd

    a = {k: np.asarray(v) for k, v in inputs.items()}
    x, c = a["x"], a["ctx_1024"]

    def chunks(w):
        return w.reshape(-1, P, w.shape[1]).transpose(1, 0, 2)

    def by_batch(w):
        return w.reshape(B, -1, P, w.shape[2]).transpose(0, 2, 1, 3).reshape(B * P, -1, w.shape[2])

    c_ab = np.zeros((B, P, 2, E), c.dtype)
    c_ab[:, :, 0] = np.tile(c[:, :K_A], (1, 2, 1))
    tail = np.zeros((B, K_B, E), c.dtype)
    tail[:, :KEYS - K_A] = c[:, K_A:]
    c_ab[:, :, 1] = np.tile(tail, (1, HH, 1))

    row = np.arange(P)
    head_mask = (row[:, None] // HD == np.arange(HH)[None, :]).astype(np.float32)
    in_pair = np.concatenate([np.arange(2 * HD) // HD, np.arange(2)])
    v_mask = np.zeros((P, 2, 2 * PAIRS, PW), np.float32)
    v_mask[:, 0] = (in_pair[None, None, :] == (row // K_A)[:, None, None])
    head = 2 * (np.arange(2 * PAIRS) % PAIRS)[:, None] + in_pair[None, :]
    v_mask[:, 1] = (head[None] == (row // K_B)[:, None, None]) & ((row % K_B) < KEYS - K_A)[:, None, None]

    vectors = ("b_out", "g1", "beta1", "b_ff2", "g2", "beta2")
    row_vectors = [a[f"L0_xattn_{n}"] for n in vectors] + [a["L1_xattn_gamma"], a["L1_xattn_beta"]]
    col_vectors = [a[f"L0_xattn_{n}"].reshape(-1, P).T for n in ("g1", "beta1", "g2", "beta2", "b_ff1")]
    arrays = {
        "x_t": by_batch(x.transpose(0, 2, 1)),
        "x_n": by_batch(x),
        "ctx_t": by_batch(c_ab.transpose(0, 3, 2, 1).reshape(B, E, 2 * P)),
        "ctx_ab": c_ab.reshape(B * P, 2, E),
        "mask0": np.broadcast_to(a["mask_Bx1x1xS2_if1"][:, 0], (B, P, KEYS)).reshape(B * P, 1, KEYS),
        "mask1": by_batch(a["mask_BxSxS2_ik1"]),
        "ident": np.eye(P, dtype=np.float32),
        "head_mask": head_mask,
        "v_mask": v_mask,
        "rows": np.broadcast_to(np.stack(row_vectors)[None], (P, 8, E)),
        "cols": np.concatenate(col_vectors, axis=1),
        "wk_rep": np.tile(a["L0_xattn_wk"].T, (1, HH)),
        "wq_rep": np.tile(a["L0_xattn_wq"].T, (1, HH)),
        "wv_rep": np.tile(a["L0_xattn_wv"].T, (HH, HH)),
        "w_out": chunks(a["L0_xattn_w_out"]),
        "w1": chunks(a["L0_xattn_w_ff1"]),
        "w2": chunks(a["L0_xattn_w_ff2"]),
        "wq1": chunks(a["L1_xattn_W_Q"].T),
        "wk1": chunks(a["L1_xattn_W_K"].T),
        "wv1": chunks(a["L1_xattn_W_V"].T),
        "wo1": chunks(a["L1_xattn_W_O"].T),
    }
    arrays = {f"in_{k}": np.ascontiguousarray(v) for k, v in arrays.items()}
    nc = bacc.Bacc("TRN2", target_bir_lowering=False, num_devices=1)
    d = {k[3:]: nc.dram_tensor(k, v.shape, mb.dt.from_np(v.dtype), kind="ExternalInput").ap() for k, v in arrays.items()}
    out = nc.dram_tensor("out", (B * P, QT, E), F32, kind="ExternalOutput").ap()
    build(nc, d, out)
    r = run_bass_kernel_spmd(nc, [arrays], core_ids=[0])
    o = r.results[0]["out"]
    return o.reshape(B, P, QT, E).transpose(0, 2, 1, 3).reshape(B, S, E)
```

```python
from contextlib import ExitStack

import concourse.bass as bass
from concourse import mybir

F32 = mybir.dt.float32
F32R = mybir.dt.float32r
BF16 = mybir.dt.bfloat16
I32 = mybir.dt.int32
ALU = mybir.AluOpType
ACT = mybir.ActivationFunctionType
AX_X = mybir.AxisListType.X

P = 128
B = 8
S = 256
KEYS = 77
E = 256
FF = 1024
HEADS = 16
HD = E // HEADS
QT = S // P
EC = E // P
FC = FF // P
HH = HEADS // EC
UNITS = QT * EC
BH = 4
K_A = 64
K_B = 16
PAIRS = HH // 2
PW = 2 * HD + 2
TCOLS = HH * (K_A + K_B)
MASKED = -1.0e20
EPS = 1e-5
SCALE = (1.0 / float(E) ** 0.5, 1.0 / float(HD) ** 0.5)


def nth(batch, per, k=0):
    return batch * per + (k + 1)


def build(nc, d, out):
    ctx = ExitStack()
    with ctx:
        def sb(name, shape, dt=F32):
            return ctx.enter_context(nc.sbuf_tensor(name, shape, dt))

        def pb(name, shape, dt=F32):
            return ctx.enter_context(nc.psum_tensor(name, shape, dt))

        def sem(name):
            return ctx.enter_context(nc.semaphore(name))

        def pair(name):
            return [sem(f"{name}_l0"), sem(f"{name}_l1")]

        ident = sb("ident", [P, P])
        ident_b = sb("ident_b", [P, P], BF16)
        head_mask = sb("head_mask", [P, HH])
        v_mask = sb("v_mask", [P, 2, 2 * PAIRS, PW])
        cols = sb("cols", [P, 4 * EC + FC])
        rows = sb("rows", [P, 8, E])
        g1c, beta1c, g2c, beta2c = (cols[:, EC * n:EC * n + EC] for n in range(4))
        bff1c = cols[:, 4 * EC:]
        b_out_r, g1_r, beta1_r, b_ff2_r, g2_r, beta2_r, gamma_r, beta_r = (rows[:, n, :] for n in range(8))
        beta1_ff2_r = sb("beta1_ff2_r", [P, E])
        wk_rep = sb("wk_rep", [HD, P])
        wq_rep = sb("wq_rep", [HD, P])
        wv_rep = sb("wv_rep", [P, P])
        wv_bd = sb("wv_bd", [P, P])
        g_bd = sb("g_bd", [P, P])
        w_out = sb("w_out", [P, EC, E])
        w_vout_s = sb("w_vout_s", [P, 2, EC, E], F32R)
        w1 = sb("w1", [P, EC, FF])
        w2 = sb("w2", [P, FC, E])
        w1_s = sb("w1_s", [P, 2, EC, FF], F32R)
        w2_s = sb("w2_s", [P, 2, FC, E], F32R)
        wq1 = sb("wq1", [P, EC, E])
        wq1_s = sb("wq1_s", [P, 2, EC, E], F32R)
        wk1 = sb("wk1", [P, EC, E])
        wv1 = sb("wv1", [P, EC, E])
        wo1 = sb("wo1", [P, EC, E])
        wo1_s = sb("wo1_s", [P, 2, EC, E], F32R)
        neg_half = sb("neg_half", [P, QT])
        eps = sb("eps", [P, QT])

        x_t = sb("x_t", [P, EC, S])
        x_s = sb("x_s", [P, 2, EC, S], F32R)
        x_n = sb("x_n", [P, QT, E])
        ctx_t = [sb(f"ctx_t{n}", [P, EC, 2 * P]) for n in range(2)]
        ctx_ab = sb("ctx_ab", [P, 2, E])
        m_i = [sb("m_i0", [P, 1, KEYS], I32), sb("m_i1", [P, QT, KEYS], I32)]
        m_bias = [sb("m_bias0", [P, 1, KEYS], BF16), sb("m_bias1", [P, QT, KEYS], BF16)]
        k_s = [sb(f"k_s{n}", [P, 2, EC, KEYS], F32R) for n in range(2)]
        k_bd = [sb(f"k_bd{n}", [P, 2, EC, HH, KEYS], F32R) for n in range(2)]
        v_bd = [sb(f"v_bd{n}", [P, 2, 2 * PAIRS, PW]) for n in range(2)]
        neg_max = sb("neg_max", [P, HH])
        diff = sb("diff", [P, HH, KEYS])
        prob = sb("prob", [P, TCOLS])
        prob_t = sb("prob_t", [P, TCOLS])
        rden = sb("rden", [P, 2 * PAIRS, 2])
        att = [sb(f"att{n}", [P, QT, E]) for n in range(2)]
        att_s = [sb(f"att_s{n}", [P, 2, EC, S], F32R) for n in range(2)]
        ysum = [sb(f"ysum{n}", [P, QT, E]) for n in range(3)]
        stats = [sb(f"stats{n}", [P, QT, 6]) for n in range(3)]
        mean_var = [sb(f"mean_var{n}", [P, QT, 2]) for n in range(3)]
        var_eps = [sb(f"var_eps{n}", [P, QT]) for n in range(3)]
        rstd = [sb(f"rstd{n}", [P, QT]) for n in range(3)]
        xhat = [sb(f"xhat{n}", [P, QT, E]) for n in range(3)]
        xn_t = [sb(f"xn_t{n}", [P, EC, S]) for n in range(2)]
        xn_s = [sb(f"xn_s{n}", [P, 2, EC, S], F32R) for n in range(2)]
        x1_res = sb("x1_res", [P, QT, E])
        h_t = sb("h_t", [P, FC, S])
        h_s = sb("h_s", [P, 2, FC, S], F32R)
        x2_res = sb("x2_res", [P, QT, E])
        q_s = sb("q_s", [P, 2, EC, S], F32R)
        o_n = sb("o_n", [P, QT, E])

        p_s = pb("p_s", [P, 2, 512])
        p_t = pb("p_t", [P, 2, 512])
        p_v = pb("p_v", [P, 512])
        ring = [pb(f"ring{n}", [P, 512]) for n in range(3)]
        pt_flat = p_t[:, :, :].rearrange("p a b -> p (a b)")[:, 0:TCOLS]
        pv_all = p_v[:, 0:2 * PAIRS * PW].rearrange("p (j c) -> p j c", c=PW)

        ld_const = sem("ld_const")
        ld_l0w = sem("ld_l0w")
        ld_rows = sem("ld_rows")
        ld_kv1w = sem("ld_kv1w")
        ld_ffw = sem("ld_ffw")
        ld_qo1w = sem("ld_qo1w")
        ld_xt = sem("ld_xt")
        ld_xn = sem("ld_xn")
        ld_ctx_t = pair("ld_ctx_t")
        ld_ctx_ab = sem("ld_ctx_ab")
        ld_mask = pair("ld_mask")
        stored = sem("stored")
        ident_b_ready = sem("ident_b_ready")
        pad_ready = sem("pad_ready")
        half_ready = sem("half_ready")
        ones_ready = sem("ones_ready")
        g_mm = sem("g_mm")
        g_ready = sem("g_ready")
        wv_bd_ready = sem("wv_bd_ready")
        wvout_mm = sem("wvout_mm")
        wvout_a_ready = sem("wvout_a_ready")
        wvout_b_ready = sem("wvout_b_ready")
        w1_split = sem("w1_split")
        w2_split = sem("w2_split")
        wq1_split = sem("wq1_split")
        wo1_split = sem("wo1_split")
        beta1_ff2_ready = sem("beta1_ff2_ready")
        k_mm = pair("k_mm")
        k_a_ready = pair("k_a_ready")
        k_b_ready = pair("k_b_ready")
        x_a_ready = sem("x_a_ready")
        x_b_ready = sem("x_b_ready")
        k_bd_ready = pair("k_bd_ready")
        v1_mm = sem("v1_mm")
        v_bd_ready = pair("v_bd_ready")
        bias_ready = pair("bias_ready")
        scores_mm = pair("scores_mm")
        max_ready = pair("max_ready")
        diff_ready = pair("diff_ready")
        prob_ready = pair("prob_ready")
        turned_mm = pair("turned_mm")
        prob_t_ready = pair("prob_t_ready")
        pv_mm = pair("pv_mm")
        rden_ready = pair("rden_ready")
        att_ready = pair("att_ready")
        att_t_mm = pair("att_t_mm")
        att_a_ready = pair("att_a_ready")
        att_b_ready = pair("att_b_ready")
        proj_mm = pair("proj_mm")
        xres_ready = sem("xres_ready")
        y_ready = [sem(f"y_ready{n}") for n in range(3)]
        stats_ready = [sem(f"stats_ready{n}") for n in range(3)]
        mv_ready = [sem(f"mv_ready{n}") for n in range(3)]
        rstd_ready = [sem(f"rstd_ready{n}") for n in range(3)]
        xhat_ready = [sem(f"xhat_ready{n}") for n in range(3)]
        x_t_mm = pair("x_t_mm")
        xn_t_ready = pair("xn_t_ready")
        xn_split = pair("xn_split")
        x1_res_ready = sem("x1_res_ready")
        x2_res_ready = sem("x2_res_ready")
        h_mm = sem("h_mm")
        h_ready = sem("h_ready")
        h_split = sem("h_split")
        ff2_mm = sem("ff2_mm")
        q_mm = sem("q_mm")
        q_a_ready = sem("q_a_ready")
        q_b_ready = sem("q_b_ready")
        o_ready = sem("o_ready")

        block = ctx.enter_context(nc.Block())

        def iterations(eng, body):
            body(0, 0, None, None)
            body(1, 1, 0, None)
            with eng.Fori(2, B - 1) as i:
                body(i, i, i - 1, i - 2)
            body(B - 1, B - 1, B - 2, B - 3)
            body(B, None, B - 1, B - 2)
            body(B + 1, None, None, B - 1)

        def more(b):
            return b is not None and not (isinstance(b, int) and b + 1 >= B)

        def later(b):
            return not (isinstance(b, int) and b == 0)

        @block.sync
        def _(sp):
            def of_batch(a, b):
                return a[bass.ds(b * P, P)] if not isinstance(b, int) else a[b * P:b * P + P]

            def load_ctx_t(layer, b):
                sp.dma_start(ctx_t[layer][:], of_batch(d["ctx_t"], b)).then_inc(ld_ctx_t[layer], 16)

            def load_mask(layer, b):
                sp.dma_start(m_i[layer][:], of_batch(d["mask0" if layer == 0 else "mask1"], b)).then_inc(ld_mask[layer], 16)

            load_ctx_t(0, 0)
            sp.dma_start(wk_rep[:], d["wk_rep"]).then_inc(ld_l0w, 16)
            sp.dma_start(wq_rep[:], d["wq_rep"]).then_inc(ld_l0w, 16)
            sp.dma_start(head_mask[:], d["head_mask"]).then_inc(ld_l0w, 16)
            sp.dma_start(ident[:], d["ident"]).then_inc(ld_const, 16)
            sp.dma_start(x_t[:], of_batch(d["x_t"], 0)).then_inc(ld_xt, 16)
            load_mask(0, 0)
            sp.dma_start(v_mask[:], d["v_mask"]).then_inc(ld_const, 16)
            sp.dma_start(ctx_ab[:], of_batch(d["ctx_ab"], 0)).then_inc(ld_ctx_ab, 16)
            sp.dma_start(wv_rep[:], d["wv_rep"]).then_inc(ld_l0w, 16)
            sp.dma_start(w_out[:], d["w_out"]).then_inc(ld_l0w, 16)
            sp.dma_start(rows[:], d["rows"]).then_inc(ld_rows, 16)
            sp.dma_start(cols[:], d["cols"]).then_inc(ld_rows, 16)
            sp.dma_start(x_n[:], of_batch(d["x_n"], 0)).then_inc(ld_xn, 16)
            sp.dma_start(w1[:], d["w1"]).then_inc(ld_ffw, 16)
            sp.dma_start(wk1[:], d["wk1"]).then_inc(ld_kv1w, 16)
            sp.dma_start(wv1[:], d["wv1"]).then_inc(ld_kv1w, 16)
            sp.dma_start(w2[:], d["w2"]).then_inc(ld_ffw, 16)
            sp.dma_start(wq1[:], d["wq1"]).then_inc(ld_qo1w, 16)
            sp.dma_start(wo1[:], d["wo1"]).then_inc(ld_qo1w, 16)

            def body(i, b, p, t):
                if more(b):
                    sp.wait_ge(x_b_ready, nth(b, 1))
                    sp.dma_start(x_t[:], of_batch(d["x_t"], b + 1)).then_inc(ld_xt, 16)
                    sp.wait_ge(k_mm[0], nth(b, 1))
                    load_ctx_t(0, b + 1)
                    sp.wait_ge(bias_ready[0], nth(b, 1))
                    load_mask(0, b + 1)
                    sp.wait_ge(v_bd_ready[0], nth(b, 1))
                    sp.dma_start(ctx_ab[:], of_batch(d["ctx_ab"], b + 1)).then_inc(ld_ctx_ab, 16)
                if b is not None:
                    if p is not None:
                        sp.wait_ge(k_mm[1], nth(p, 1))
                        sp.wait_ge(v1_mm, nth(p, 2, 1))
                    load_ctx_t(1, b)
                    if p is not None:
                        sp.wait_ge(bias_ready[1], nth(p, 1))
                    load_mask(1, b)
                if t is not None:
                    sp.wait_ge(o_ready, nth(t, 2, 1))
                    sp.dma_start(of_batch(out, t), o_n[:]).then_inc(stored, 16)
                if more(b):
                    sp.wait_ge(y_ready[0], nth(b, 1))
                    sp.dma_start(x_n[:], of_batch(d["x_n"], b + 1)).then_inc(ld_xn, 16)

            iterations(sp, body)
            sp.wait_ge(stored, 16 * B)

        @block.tensor
        def _(pe):
            q_of = [x_s, q_s]

            def products(o, lhs, rhs, start, stop):
                for n, (l, r) in enumerate(((0, 0), (0, 1), (1, 0))):
                    last = pe.matmul(o, lhs(l), rhs(r), start=start and n == 0, stop=stop and n == 2)
                return last

            def scores(layer, b, u, before):
                qt, half = u // EC, u % EC
                if u == 0:
                    if layer == 0:
                        pe.wait_ge(x_b_ready, nth(b, 1))
                    else:
                        pe.wait_ge(q_b_ready, nth(b, 1))
                    pe.wait_ge(bias_ready[layer], nth(b, 1))
                if qt == 0:
                    pe.wait_ge(k_bd_ready[layer], nth(b, 2 * EC, 2 * half + 1))
                if before is not None:
                    pe.wait_ge(diff_ready[before[0]], nth(before[1], UNITS, before[2]))
                for n in range(2):
                    o = p_s[:, n, 0:BH * KEYS]
                    bias = m_bias[layer][:, qt if layer else 0, :].unsqueeze(1).to_broadcast((P, BH, KEYS))
                    pe.matmul(o, ident_b[:], bias, start=True, stop=False)
                    last = products(o, lambda l: q_of[layer][:, l, half, qt * P:(qt + 1) * P],
                                    lambda r: k_bd[layer][:, r, half, n * BH:(n + 1) * BH, :], False, True)
                last.then_inc(scores_mm[layer], 1)

            def turn(layer, b, u, before):
                pe.wait_ge(prob_ready[layer], nth(b, UNITS, u))
                if before is not None:
                    pe.wait_ge(prob_t_ready[before[0]], nth(before[1], UNITS, before[2]))
                for j in range(PAIRS):
                    pe.transpose(p_t[:, 0, j * P:(j + 1) * P], prob[:, j * P:(j + 1) * P], ident[:])
                pe.transpose(p_t[:, 1, 0:P], prob[:, PAIRS * P:], ident[:]).then_inc(turned_mm[layer], 1)

            def values(layer, b, u, before):
                half = u % EC
                pe.wait_ge(prob_t_ready[layer], nth(b, UNITS, u))
                if u == 0:
                    pe.wait_ge(v_bd_ready[layer], nth(b, 1))
                if half == 0 and before is not None:
                    pe.wait_ge(att_ready[before[0]], nth(before[1], QT, before[2] // EC))
                for j in range(PAIRS):
                    pe.matmul(pv_all[:, half * PAIRS + j, :], prob_t[:, j * P:(j + 1) * P],
                              v_bd[layer][:, 0, half * PAIRS + j, :], start=(half == 0 and j == 0), stop=False,
                              skip_group_check=True)
                pe.matmul(pv_all[:, half * PAIRS:(half + 1) * PAIRS, :], prob_t[:, PAIRS * P:],
                          v_bd[layer][:, 1, half * PAIRS:(half + 1) * PAIRS, :], start=False, stop=True,
                          skip_group_check=True).then_inc(pv_mm[layer], 1)

            def keys(layer, b, bank):
                pe.wait_ge(ld_ctx_t[layer], 16 * b + 16)
                c_t = ctx_t[layer][:, :, K_A:K_A + KEYS]
                for m in range(EC):
                    o = bank[:, m * KEYS:(m + 1) * KEYS]
                    if layer == 0:
                        last = pe.matmul(o, g_bd[:], c_t[:, m, :], start=True, stop=True)
                    else:
                        for c in range(EC):
                            last = pe.matmul(o, wk1[:, c, m * P:(m + 1) * P], c_t[:, c, :],
                                             start=(c == 0), stop=(c == EC - 1))
                last.then_inc(k_mm[layer], 1)

            def values_1(b, part, bank):
                for c in range(EC):
                    last = pe.matmul(bank[:, part * E:(part + 1) * E], ctx_t[1][:, c, part * P:(part + 1) * P], wv1[:, c, :],
                                     start=(c == 0), stop=(c == EC - 1))
                last.then_inc(v1_mm, 1)

            def turn_rows(src, bank):
                for c in range(EC):
                    for qt in range(QT):
                        last = pe.transpose(bank[:, c * S + qt * P:c * S + (qt + 1) * P],
                                            src[:, qt, c * P:(c + 1) * P], ident[:])
                return last

            def to_rows(lhs, w, chunks, bank, qt):
                for c in range(chunks):
                    last = products(bank[:, qt * E:(qt + 1) * E], lambda l: lhs[:, l, c, qt * P:(qt + 1) * P],
                                    lambda r: w[:, r, c, :], c == 0, c == chunks - 1)
                return last

            def to_columns(w, m, rhs, o):
                for c in range(EC):
                    last = products(o, lambda l: w[:, l, c, m * P:(m + 1) * P], lambda r: rhs[:, r, c, :],
                                    c == 0, c == EC - 1)
                return last

            def attention_out(layer, b, bank):
                pe.wait_ge(att_ready[layer], nth(b, QT, QT - 1))
                turn_rows(att[layer], bank).then_inc(att_t_mm[layer], 1)

            def project(layer, b, bank):
                pe.wait_ge(att_b_ready[layer], nth(b, 1))
                for qt in range(QT):
                    last = to_rows(att_s[layer], (w_vout_s, wo1_s)[layer], EC, bank, qt)
                last.then_inc(proj_mm[layer], 1)

            def normed_to_columns(n, b, bank):
                pe.wait_ge(xhat_ready[n], nth(b, QT, QT - 1))
                turn_rows(xhat[n], bank).then_inc(x_t_mm[n], 1)

            def ff1(b, g, bank):
                if g == 0:
                    pe.wait_ge(xn_split[0], nth(b, 2, 1))
                for f in (2 * g, 2 * g + 1):
                    last = to_columns(w1_s, f, xn_s[0], bank[:, (f % 2) * S:(f % 2 + 1) * S])
                last.then_inc(h_mm, 1)

            def query_1(b, bank):
                pe.wait_ge(xn_split[1], nth(b, 2, 1))
                for m in range(EC):
                    last = to_columns(wq1_s, m, xn_s[1], bank[:, m * S:(m + 1) * S])
                last.then_inc(q_mm, 1)

            pe.wait_ge(ld_l0w, 16 * 5)
            pe.matmul(ring[0][:, 0:P], wk_rep[:], wq_rep[:], start=True, stop=True).then_inc(g_mm, 1)
            pe.wait_ge(g_ready, 1)
            keys(0, 0, ring[2])
            pe.wait_ge(wv_bd_ready, 1)
            for c in range(EC):
                last = pe.matmul(ring[1][:, c * E:(c + 1) * E], wv_bd[:], w_out[:, c, :], start=True, stop=True)
            last.then_inc(wvout_mm, 1)
            pe.wait_ge(ident_b_ready, 1)
            pe.wait_ge(ld_const, 32)

            def body(i, b, p, t):
                unit = [(0, b, u) if b is not None else None for u in range(UNITS)]
                unit += [(1, p, u) if p is not None else None for u in range(UNITS)]
                older = [(1, t, u) if t is not None else (0, p, u) if p is not None else None for u in (UNITS - 2, UNITS - 1)]
                seq = older + unit

                def s_(s):
                    if unit[s] is not None:
                        scores(*unit[s], seq[s + 1])

                def t_(s):
                    if seq[s + 1] is not None and not (s == 0 and t is None):
                        turn(*seq[s + 1], seq[s])

                def v_(s):
                    if seq[s + 1] is None or (s == 0 and t is None):
                        return
                    tile_before = seq[s] if s else None
                    values(*seq[s + 1], tile_before)

                s_(0)
                t_(0)
                if p is not None:
                    if not later(p):
                        pe.wait_ge(ld_kv1w, 32)
                    pe.wait_ge(xn_t_ready[0], nth(p, 1))
                    keys(1, p, ring[0])
                    for g in (2, 3):
                        pe.wait_ge(h_ready, nth(p, FC, 2 * g - 3))
                        ff1(p, g, ring[g - 1])
                v_(0)
                s_(1)
                t_(1)
                if p is not None:
                    if not later(p):
                        pe.wait_ge(w2_split, 2)
                    pe.wait_ge(k_b_ready[1], nth(p, 1))
                    pe.wait_ge(h_split, nth(p, FC, FC - 1))
                    to_rows(h_s, w2_s, FC, ring[0], 0)
                v_(1)
                if p is not None:
                    to_rows(h_s, w2_s, FC, ring[0], 1).then_inc(ff2_mm, 1)
                t_(2)
                s_(2)
                if t is not None:
                    attention_out(1, t, ring[1])
                v_(2)
                s_(3)
                t_(3)
                if p is not None:
                    normed_to_columns(1, p, ring[2])
                    pe.wait_ge(y_ready[1], nth(p, 1))
                    pe.wait_ge(ld_ctx_t[1], 16 * p + 16)
                    values_1(p, 0, ring[0])
                v_(3)
                if p is not None:
                    if not later(p):
                        pe.wait_ge(wq1_split, 2)
                    if t is not None:
                        pe.wait_ge(att_b_ready[1], nth(t, 1))
                    query_1(p, ring[1])
                t_(4)
                if p is not None:
                    values_1(p, 1, ring[0])
                if more(b):
                    if p is not None:
                        pe.wait_ge(xn_t_ready[1], nth(p, 1))
                    keys(0, b + 1, ring[2])
                v_(4)
                s_(4)
                if b is not None:
                    if p is not None:
                        pe.wait_ge(v_bd_ready[1], nth(p, 1))
                    attention_out(0, b, ring[0])
                if t is not None:
                    if not later(t):
                        pe.wait_ge(wo1_split, 2)
                    if p is not None:
                        pe.wait_ge(q_b_ready, nth(p, 1))
                    project(1, t, ring[1])
                s_(5)
                t_(5)
                if b is not None:
                    if not later(b):
                        pe.wait_ge(wvout_b_ready, 1)
                    if more(b):
                        pe.wait_ge(k_b_ready[0], nth(b + 1, 1))
                    project(0, b, ring[2])
                v_(5)
                t_(6)
                s_(6)
                v_(6)
                if b is not None:
                    normed_to_columns(0, b, ring[0])
                s_(7)
                t_(7)
                v_(7)
                if b is not None:
                    if not later(b):
                        pe.wait_ge(w1_split, 2)
                    if t is not None:
                        pe.wait_ge(y_ready[2], nth(t, 1))
                    ff1(b, 0, ring[1])
                    pe.wait_ge(y_ready[0], nth(b, 1))
                    ff1(b, 1, ring[2])

            iterations(pe, body)

        @block.vector
        def _(dve):
            def bias_of(layer, b):
                dve.wait_ge(ld_mask[layer], 16 * b + 16)
                dve.tensor_scalar(m_bias[layer][:], m_i[layer][:], float(layer), MASKED, ALU.is_equal, ALU.mult)\
                   .then_inc(bias_ready[layer], 1)

            def flat(a):
                return a.rearrange("p c q -> p (c q)")

            def low_part(split, src, a_ready, count, done):
                dve.wait_ge(a_ready, count)
                dve.tensor_tensor(flat(split[:, 1]), src, flat(split[:, 0]).bitcast(F32), ALU.subtract).then_inc(done, 1)

            def split(dst, src, done, count):
                dve.tensor_copy(dst[0], src).then_inc(done, 1)
                dve.wait_ge(done, count)
                dve.tensor_tensor(dst[1], src, dst[0].bitcast(F32), ALU.subtract).then_inc(done, 1)

            def split_weight(dst, src, loaded, count, done):
                dve.wait_ge(loaded, count)
                split([flat(dst[:, n]) for n in range(2)], flat(src[:]), done, 1)

            dve.memset(prob[:, HH * K_A:], 0.0).then_inc(pad_ready, 1)
            dve.wait_ge(ld_l0w, 16 * 5)
            by_head = head_mask[:].unsqueeze(2).to_broadcast((P, HH, HD))
            dve.tensor_tensor(wv_bd[:].rearrange("p (h c) -> p h c", h=HH), wv_rep[:].rearrange("p (h c) -> p h c", h=HH),
                              by_head, ALU.mult).then_inc(wv_bd_ready, 1)
            dve.wait_ge(g_mm, 1)
            dve.tensor_tensor(g_bd[:].rearrange("p (h c) -> p h c", h=HH), ring[0][:, 0:P].rearrange("p (h c) -> p h c", h=HH),
                              by_head, ALU.mult).then_inc(g_ready, 1)
            dve.wait_ge(ld_const, 32)
            low_part(k_s[0], ring[2][:, 0:EC * KEYS], k_a_ready[0], 1, k_b_ready[0])
            dve.tensor_copy(ident_b[:], ident[:]).then_inc(ident_b_ready, 1)
            bias_of(0, 0)
            for layer in range(2):
                dve.tensor_copy(v_bd[layer][:, :, :, 2 * HD:], v_mask[:, :, :, 2 * HD:]).then_inc(ones_ready, 1)
            dve.wait_ge(ones_ready, 2)
            low_part(w_vout_s, ring[1][:], wvout_a_ready, 1, wvout_b_ready)

            def shifted(layer, b, u, before):
                dve.wait_ge(scores_mm[layer], nth(b, UNITS, u))
                four = p_s[:, :, 0:BH * KEYS].rearrange("p n (h k) -> p n h k", h=BH)
                dve.tensor_reduce(neg_max[:].rearrange("p (n h) -> p n h", n=2), four, AX_X, ALU.max,
                                  negate=True).then_inc(max_ready[layer], 1)
                dve.wait_ge(max_ready[layer], nth(b, UNITS, u))
                if before is not None:
                    dve.wait_ge(prob_ready[before[0]], nth(before[1], UNITS, before[2]))
                dve.tensor_tensor(diff[:].rearrange("p (n h) k -> p n h k", n=2), four,
                                  neg_max[:].rearrange("p (n h) -> p n h", n=2).unsqueeze(3).to_broadcast((P, 2, BH, KEYS)),
                                  ALU.add).then_inc(diff_ready[layer], 1)

            def normalise(layer, b, qt):
                dve.wait_ge(pv_mm[layer], nth(b, UNITS, qt * EC + EC - 1))
                dve.reciprocal(rden[:], pv_all[:, :, 2 * HD:]).then_inc(rden_ready[layer], 1)
                dve.wait_ge(rden_ready[layer], nth(b, QT, qt))
                dve.tensor_tensor(att[layer][:, qt, :].rearrange("p (j h c) -> p j h c", h=2, c=HD),
                                  pv_all[:, :, 0:2 * HD].rearrange("p j (h c) -> p j h c", h=2),
                                  rden[:].unsqueeze(3).to_broadcast((P, 2 * PAIRS, 2, HD)), ALU.mult)\
                   .then_inc(att_ready[layer], 1)

            def sum_and_stats(n, b, bank, res):
                dve.tensor_tensor(ysum[n][:].rearrange("p q e -> p (q e)"), bank[:], res[:].rearrange("p q e -> p (q e)"),
                                  ALU.add).then_inc(y_ready[n], 1)
                dve.wait_ge(y_ready[n], nth(b, 1))
                for qt in range(QT):
                    dve.bn_stats(stats[n][:, qt, :], ysum[n][:, qt, :]).then_inc(stats_ready[n], 1)
                dve.drain()
                for qt in range(QT):
                    dve.bn_aggr(mean_var[n][:, qt, :], stats[n][:, qt, :]).then_inc(mv_ready[n], 1)

            def normed(n, b):
                dve.wait_ge(rstd_ready[n], nth(b, 2, 1))
                for qt in range(QT):
                    dve.tensor_scalar(xhat[n][:, qt, :], ysum[n][:, qt, :], mean_var[n][:, qt, 0:1],
                                      rstd[n][:, qt:qt + 1], ALU.subtract, ALU.mult).then_inc(xhat_ready[n], 1)

            def split_hidden(b, g):
                dve.wait_ge(h_ready, nth(b, FC, 2 * g + 1))
                split([flat(h_s[:, n, 2 * g:2 * g + 2]) for n in range(2)], flat(h_t[:, 2 * g:2 * g + 2]),
                      h_split, nth(b, FC, 2 * g))

            def split_normed(n, b):
                dve.wait_ge(xn_t_ready[n], nth(b, 1))
                split([flat(xn_s[n][:, m]) for m in range(2)], flat(xn_t[n][:]), xn_split[n], nth(b, 2, 0))

            def body(i, b, p, t):
                unit = [(0, b, u) if b is not None else None for u in range(UNITS)]
                unit += [(1, p, u) if p is not None else None for u in range(UNITS)]
                seq = [(1, t, UNITS - 1) if t is not None else (0, p, UNITS - 1) if p is not None else None] + unit

                def d_(s):
                    if unit[s] is not None:
                        shifted(*unit[s], seq[s])

                if p is not None:
                    split_hidden(p, 0)
                d_(0)
                if p is not None:
                    low_part(k_s[1], ring[0][:, 0:EC * KEYS], k_a_ready[1], nth(p, 1), k_b_ready[1])
                    split_hidden(p, 1)
                    split_hidden(p, 2)
                if p is not None:
                    split_hidden(p, 3)
                d_(1)
                if t is not None:
                    normalise(1, t, 1)
                if p is not None:
                    if later(p):
                        dve.wait_ge(scores_mm[1], nth(p - 1, UNITS, UNITS - 1))
                    bias_of(1, p)
                if p is not None:
                    if not later(p):
                        split_weight(wq1_s, wq1, ld_qo1w, 32, wq1_split)
                        split_weight(wo1_s, wo1, ld_qo1w, 32, wo1_split)
                    dve.wait_ge(ff2_mm, nth(p, 1))
                    dve.wait_ge(x1_res_ready, nth(p, 2, 1))
                    sum_and_stats(1, p, ring[0], x1_res)
                d_(2)
                if t is not None:
                    low_part(att_s[1], ring[1][:], att_a_ready[1], nth(t, 1), att_b_ready[1])
                if p is not None:
                    if later(p):
                        dve.wait_ge(x2_res_ready, nth(p - 1, 2, 1))
                    normed(1, p)
                if b is not None:
                    normalise(0, b, 0)
                d_(3)
                if p is not None:
                    split_normed(1, p)
                if p is not None:
                    low_part(q_s, ring[1][:], q_a_ready, nth(p, 1), q_b_ready)
                    dve.wait_ge(v1_mm, nth(p, 2, 1))
                    dve.tensor_tensor(v_bd[1][:, :, :, 0:2 * HD], ring[0][:].rearrange("p (a j c) -> p a j c", a=2, c=2 * HD),
                                      v_mask[:, :, :, 0:2 * HD], ALU.mult).then_inc(v_bd_ready[1], 1)
                if more(b):
                    low_part(k_s[0], ring[2][:, 0:EC * KEYS], k_a_ready[0], nth(b + 1, 1), k_b_ready[0])
                    dve.wait_ge(scores_mm[0], nth(b, UNITS, UNITS - 1))
                    bias_of(0, b + 1)
                if b is not None:
                    normalise(0, b, 1)
                d_(4)
                if b is not None:
                    low_part(att_s[0], ring[0][:], att_a_ready[0], nth(b, 1), att_b_ready[0])
                if not later(b) and b is not None:
                    split_weight(w1_s, w1, ld_ffw, 32, w1_split)
                if t is not None:
                    dve.wait_ge(proj_mm[1], nth(t, 1))
                    dve.wait_ge(x2_res_ready, nth(t, 2, 1))
                    sum_and_stats(2, t, ring[1], x2_res)
                d_(5)
                if b is not None:
                    dve.wait_ge(proj_mm[0], nth(b, 1))
                    dve.wait_ge(xres_ready, nth(b, 1))
                    sum_and_stats(0, b, ring[2], x_n)
                d_(6)
                if b is not None:
                    normed(0, b)
                if t is not None:
                    if later(t):
                        dve.wait_ge(o_ready, nth(t - 1, 2, 1))
                    normed(2, t)
                if p is not None:
                    normalise(1, p, 0)
                if not later(b) and b is not None:
                    split_weight(w2_s, w2, ld_ffw, 32, w2_split)
                if b is not None:
                    split_normed(0, b)
                d_(7)

            iterations(dve, body)

        @block.scalar
        def _(act):
            def exponential(layer, b, u, before):
                act.wait_ge(diff_ready[layer], nth(b, UNITS, u))
                if before is not None:
                    act.wait_ge(turned_mm[before[0]], nth(before[1], UNITS, before[2]))
                act.activation(prob[:, 0:HH * K_A].rearrange("p (h k) -> p h k", h=HH), diff[:, :, 0:K_A], ACT.Exp,
                               scale=SCALE[layer])
                act.activation(prob[:, HH * K_A:].rearrange("p (h k) -> p h k", h=HH)[:, :, 0:KEYS - K_A],
                               diff[:, :, K_A:], ACT.Exp, scale=SCALE[layer]).then_inc(prob_ready[layer], 1)

            def copy_turned(layer, b, u, before):
                act.wait_ge(turned_mm[layer], nth(b, UNITS, u))
                if before is not None:
                    act.wait_ge(pv_mm[before[0]], nth(before[1], UNITS, before[2]))
                act.activation(prob_t[:], pt_flat, ACT.Copy).then_inc(prob_t_ready[layer], 1)

            def high_part(split, src, produced, count, done):
                act.wait_ge(produced, count)
                act.activation(split[:, 0].rearrange("p c q -> p (c q)"), src, ACT.Copy).then_inc(done, 1)

            def scaled(n, b, bank, g, beta):
                act.wait_ge(x_t_mm[n], nth(b, 1))
                for c in range(EC):
                    last = act.activation(xn_t[n][:, c, :], bank[:, c * S:(c + 1) * S], ACT.Identity,
                                          bias=beta[:, c:c + 1], scale=g[:, c:c + 1])
                last.then_inc(xn_t_ready[n], 1)

            def hidden(b, g, bank):
                act.wait_ge(h_mm, nth(b, FC // 2, g))
                for f in (2 * g, 2 * g + 1):
                    act.activation(h_t[:, f, :], bank[:, (f % 2) * S:(f % 2 + 1) * S], ACT.Relu,
                                   bias=bff1c[:, f:f + 1]).then_inc(h_ready, 1)

            high_part(x_s, x_t[:].rearrange("p c q -> p (c q)"), ld_xt, 16, x_a_ready)
            high_part(k_s[0], ring[2][:, 0:EC * KEYS], k_mm[0], 1, k_a_ready[0])
            high_part(w_vout_s, ring[1][:], wvout_mm, 1, wvout_a_ready)
            act.wait_ge(ld_rows, 32)
            act.wait_ge(pad_ready, 1)

            def body(i, b, p, t):
                unit = [(0, b, u) if b is not None else None for u in range(UNITS)]
                unit += [(1, p, u) if p is not None else None for u in range(UNITS)]
                older = [(1, t, u) if t is not None else (0, p, u) if p is not None else None for u in (UNITS - 2, UNITS - 1)]
                seq = older + unit

                def c_(s):
                    if seq[s + 1] is not None and not (s == 0 and t is None):
                        copy_turned(*seq[s + 1], seq[s])

                def e_(s):
                    if unit[s] is not None:
                        exponential(*unit[s], seq[s + 1])

                if p is not None:
                    hidden(p, 0, ring[1])
                    hidden(p, 1, ring[2])
                c_(0)
                if p is not None:
                    high_part(k_s[1], ring[0][:, 0:EC * KEYS], k_mm[1], nth(p, 1), k_a_ready[1])
                e_(0)
                if p is not None:
                    hidden(p, 2, ring[1])
                    hidden(p, 3, ring[2])
                c_(1)
                e_(1)
                c_(2)
                if t is not None:
                    high_part(att_s[1], ring[1][:], att_t_mm[1], nth(t, 1), att_a_ready[1])
                e_(2)
                c_(3)
                if p is not None:
                    scaled(1, p, ring[2], g2c, beta2c)
                e_(3)
                if p is not None:
                    high_part(q_s, ring[1][:], q_mm, nth(p, 1), q_a_ready)
                c_(4)
                if more(b):
                    high_part(k_s[0], ring[2][:, 0:EC * KEYS], k_mm[0], nth(b + 1, 1), k_a_ready[0])
                    act.wait_ge(scores_mm[0], nth(b, UNITS, UNITS - 1))
                    high_part(x_s, x_t[:].rearrange("p c q -> p (c q)"), ld_xt, 16 * b + 32, x_a_ready)
                if b is not None:
                    high_part(att_s[0], ring[0][:], att_t_mm[0], nth(b, 1), att_a_ready[0])
                e_(4)
                c_(5)
                e_(5)
                c_(6)
                e_(6)
                if b is not None:
                    scaled(0, b, ring[0], g1c, beta1c)
                c_(7)
                e_(7)

            iterations(act, body)

        @block.gpsimd
        def _(pool):
            def low_x(b):
                pool.wait_ge(x_a_ready, nth(b, 1))
                pool.tensor_tensor(x_s[:, 1], x_t[:], x_s[:, 0].bitcast(F32), ALU.subtract).then_inc(x_b_ready, 1)

            def block_keys(layer, b):
                wide = (P, HH, KEYS)
                for c in range(EC):
                    for n in range(2):
                        if c == 0:
                            pool.wait_ge((k_a_ready, k_b_ready)[n][layer], nth(b, 1))
                        pool.tensor_tensor(k_bd[layer][:, n, c], k_s[layer][:, n, c, :].bitcast(F32).unsqueeze(1).to_broadcast(wide),
                                           head_mask[:].unsqueeze(2).to_broadcast(wide), ALU.mult)\
                            .then_inc(k_bd_ready[layer], 1)

            def block_values_0(b):
                pool.wait_ge(ld_ctx_ab, 16 * b + 16)
                pool.tensor_tensor(v_bd[0][:, :, :, 0:2 * HD], ctx_ab[:].rearrange("p a (j c) -> p a j c", c=2 * HD),
                                   v_mask[:, :, :, 0:2 * HD], ALU.mult).then_inc(v_bd_ready[0], 1)

            def inverse_deviation(n, b):
                pool.wait_ge(mv_ready[n], nth(b, QT, QT - 1))
                pool.tensor_tensor(var_eps[n][:], mean_var[n][:, :, 1], eps[:], ALU.add).then_inc(rstd_ready[n], 1)
                pool.wait_ge(rstd_ready[n], nth(b, 2, 0))
                pool.tensor_tensor(rstd[n][:], var_eps[n][:], neg_half[:], ALU.pow).then_inc(rstd_ready[n], 1)

            def gain_and_shift(n, b, dst, g, shift, done):
                pool.wait_ge(xhat_ready[n], nth(b, QT, QT - 1))
                wide = (P, QT, E)
                pool.tensor_tensor(dst[:], xhat[n][:], g.unsqueeze(1).to_broadcast(wide), ALU.mult).then_inc(done, 1)
                pool.wait_ge(done, nth(b, 2, 0))
                pool.tensor_tensor(dst[:], dst[:], shift.unsqueeze(1).to_broadcast(wide), ALU.add).then_inc(done, 1)

            pool.memset(neg_half[:], -0.5).then_inc(half_ready, 1)
            pool.memset(eps[:], EPS).then_inc(half_ready, 1)
            pool.wait_ge(half_ready, 2)
            pool.wait_ge(ld_l0w, 16 * 5)
            low_x(0)
            block_keys(0, 0)
            pool.wait_ge(ld_const, 32)
            pool.wait_ge(ones_ready, 2)
            block_values_0(0)
            pool.wait_ge(ld_rows, 32)
            pool.tensor_tensor(beta1_ff2_r[:], beta1_r, b_ff2_r, ALU.add).then_inc(beta1_ff2_ready, 1)
            pool.wait_ge(beta1_ff2_ready, 1)

            def body(i, b, p, t):
                if p is not None:
                    if later(p):
                        pool.wait_ge(scores_mm[1], nth(p - 1, UNITS, UNITS - 1))
                    block_keys(1, p)
                if b is not None:
                    pool.wait_ge(ld_xn, 16 * b + 16)
                    pool.tensor_tensor(x_n[:], x_n[:], b_out_r.unsqueeze(1).to_broadcast((P, QT, E)), ALU.add)\
                        .then_inc(xres_ready, 1)
                if p is not None:
                    inverse_deviation(1, p)
                if more(b):
                    pool.wait_ge(scores_mm[0], nth(b, UNITS, UNITS - 1))
                    low_x(b + 1)
                    block_keys(0, b + 1)
                if b is not None:
                    inverse_deviation(0, b)
                if t is not None:
                    inverse_deviation(2, t)
                if more(b):
                    pool.wait_ge(pv_mm[0], nth(b, UNITS, UNITS - 1))
                    block_values_0(b + 1)
                if p is not None:
                    if later(p):
                        pool.wait_ge(y_ready[2], nth(p - 1, 1))
                    gain_and_shift(1, p, x2_res, g2_r, beta2_r, x2_res_ready)
                if b is not None:
                    if p is not None:
                        pool.wait_ge(y_ready[1], nth(p, 1))
                    gain_and_shift(0, b, x1_res, g1_r, beta1_ff2_r[:], x1_res_ready)
                if t is not None:
                    if later(t):
                        pool.wait_ge(stored, 16 * t)
                    gain_and_shift(2, t, o_n, gamma_r, beta_r, o_ready)

            iterations(pool, body)


def kernel(**inputs):
    import numpy as np
    import concourse.bacc as bacc
    from concourse import mybir as mb
    from concourse.bass_utils import run_bass_kernel_spmd

    a = {k: np.asarray(v) for k, v in inputs.items()}
    x, c = a["x"], a["ctx_1024"]

    def chunks(w):
        return w.reshape(-1, P, w.shape[1]).transpose(1, 0, 2)

    def by_batch(w):
        return w.reshape(B, -1, P, w.shape[2]).transpose(0, 2, 1, 3).reshape(B * P, -1, w.shape[2])

    c_ab = np.zeros((B, P, 2, E), c.dtype)
    c_ab[:, :, 0] = np.tile(c[:, :K_A], (1, 2, 1))
    tail = np.zeros((B, K_B, E), c.dtype)
    tail[:, :KEYS - K_A] = c[:, K_A:]
    c_ab[:, :, 1] = np.tile(tail, (1, HH, 1))

    row = np.arange(P)
    head_mask = (row[:, None] // HD == np.arange(HH)[None, :]).astype(np.float32)
    in_pair = np.concatenate([np.arange(2 * HD) // HD, np.arange(2)])
    v_mask = np.zeros((P, 2, 2 * PAIRS, PW), np.float32)
    v_mask[:, 0] = (in_pair[None, None, :] == (row // K_A)[:, None, None])
    head = 2 * (np.arange(2 * PAIRS) % PAIRS)[:, None] + in_pair[None, :]
    v_mask[:, 1] = (head[None] == (row // K_B)[:, None, None]) & ((row % K_B) < KEYS - K_A)[:, None, None]

    vectors = ("b_out", "g1", "beta1", "b_ff2", "g2", "beta2")
    row_vectors = [a[f"L0_xattn_{n}"] for n in vectors] + [a["L1_xattn_gamma"], a["L1_xattn_beta"]]
    col_vectors = [a[f"L0_xattn_{n}"].reshape(-1, P).T for n in ("g1", "beta1", "g2", "beta2", "b_ff1")]
    arrays = {
        "x_t": by_batch(x.transpose(0, 2, 1)),
        "x_n": by_batch(x),
        "ctx_t": by_batch(c_ab.transpose(0, 3, 2, 1).reshape(B, E, 2 * P)),
        "ctx_ab": c_ab.reshape(B * P, 2, E),
        "mask0": np.broadcast_to(a["mask_Bx1x1xS2_if1"][:, 0], (B, P, KEYS)).reshape(B * P, 1, KEYS),
        "mask1": by_batch(a["mask_BxSxS2_ik1"]),
        "ident": np.eye(P, dtype=np.float32),
        "head_mask": head_mask,
        "v_mask": v_mask,
        "rows": np.broadcast_to(np.stack(row_vectors)[None], (P, 8, E)),
        "cols": np.concatenate(col_vectors, axis=1),
        "wk_rep": np.tile(a["L0_xattn_wk"].T, (1, HH)),
        "wq_rep": np.tile(a["L0_xattn_wq"].T, (1, HH)),
        "wv_rep": np.tile(a["L0_xattn_wv"].T, (HH, HH)),
        "w_out": chunks(a["L0_xattn_w_out"]),
        "w1": chunks(a["L0_xattn_w_ff1"]),
        "w2": chunks(a["L0_xattn_w_ff2"]),
        "wq1": chunks(a["L1_xattn_W_Q"].T),
        "wk1": chunks(a["L1_xattn_W_K"].T),
        "wv1": chunks(a["L1_xattn_W_V"].T),
        "wo1": chunks(a["L1_xattn_W_O"].T),
    }
    arrays = {f"in_{k}": np.ascontiguousarray(v) for k, v in arrays.items()}
    nc = bacc.Bacc("TRN2", target_bir_lowering=False, num_devices=1)
    d = {k[3:]: nc.dram_tensor(k, v.shape, mb.dt.from_np(v.dtype), kind="ExternalInput").ap() for k, v in arrays.items()}
    out = nc.dram_tensor("out", (B * P, QT, E), F32, kind="ExternalOutput").ap()
    build(nc, d, out)
    r = run_bass_kernel_spmd(nc, [arrays], core_ids=[0])
    o = r.results[0]["out"]
    return o.reshape(B, P, QT, E).transpose(0, 2, 1, 3).reshape(B, S, E)
```

```python
from contextlib import ExitStack

import concourse.bass as bass
from concourse import mybir

F32 = mybir.dt.float32
F32R = mybir.dt.float32r
BF16 = mybir.dt.bfloat16
I32 = mybir.dt.int32
ALU = mybir.AluOpType
ACT = mybir.ActivationFunctionType
AX_X = mybir.AxisListType.X

P = 128
B = 8
S = 256
KEYS = 77
E = 256
FF = 1024
HEADS = 16
HD = E // HEADS
QT = S // P
EC = E // P
FC = FF // P
HH = HEADS // EC
UNITS = QT * EC
BANKS = 2
BH = HH // BANKS
K_A = 64
K_B = 16
PAIRS = HH // 2
SIDE = BH * HD
PW = 2 * HD + 2
TCOLS = HH * (K_A + K_B)
MASKED = -1.0e20
EPS = 1e-5
SCALE = (1.0 / float(E) ** 0.5, 1.0 / float(HD) ** 0.5)


def nth(batch, per, k=0):
    return batch * per + (k + 1)


def build(nc, d, out):
    ctx = ExitStack()
    with ctx:
        def sb(name, shape, dt=F32):
            return ctx.enter_context(nc.sbuf_tensor(name, shape, dt))

        def pb(name, shape, dt=F32):
            return ctx.enter_context(nc.psum_tensor(name, shape, dt))

        def sem(name):
            return ctx.enter_context(nc.semaphore(name))

        def pair(name):
            return [sem(f"{name}_l0"), sem(f"{name}_l1")]

        ident = sb("ident", [P, P])
        ident_b = sb("ident_b", [P, P], BF16)
        head_mask = sb("head_mask", [P, HH])
        side_mask = sb("side_mask", [P, BH])
        v_mask = sb("v_mask", [P, 2, 2 * PAIRS, PW])
        cols = sb("cols", [P, 4 * EC + FC])
        rows = sb("rows", [P, 8, E])
        g1c, beta1c, g2c, beta2c = (cols[:, EC * n:EC * n + EC] for n in range(4))
        b_ff1c = cols[:, 4 * EC:]
        shift_cols = sb("shift_cols", [P, FC + EC])
        h_shift, q_shift = shift_cols[:, 0:FC], shift_cols[:, FC:]
        b_out_r, g1_r, beta1_r, b_ff2_r, g2_r, beta2_r, gamma_r, beta_r = (rows[:, n, :] for n in range(8))
        beta1_ff2_r = sb("beta1_ff2_r", [P, E])
        wk_rep = sb("wk_rep", [HD, P])
        wq_rep = sb("wq_rep", [HD, P])
        wv_rep = sb("wv_rep", [P, P])
        wv_bd = sb("wv_bd", [P, P])
        g_bd = sb("g_bd", [P, BANKS, 2, SIDE])
        w_out = sb("w_out", [P, EC, E])
        w_vout_s = sb("w_vout_s", [P, 2, EC, E], F32R)
        w1 = sb("w1", [P, EC, FF])
        w2 = sb("w2", [P, FC, E])
        w1_s = sb("w1_s", [P, 2, EC, FF], F32R)
        w2_s = sb("w2_s", [P, 2, FC, E], F32R)
        wq1 = sb("wq1", [P, EC, E])
        wq1_s = sb("wq1_s", [P, 2, EC, E], F32R)
        wk1 = sb("wk1", [P, EC, E])
        wv1 = sb("wv1", [P, EC, E])
        wv1_s = sb("wv1_s", [P, 2, EC, E], F32R)
        wo1 = sb("wo1", [P, EC, E])
        wo1_s = sb("wo1_s", [P, 2, EC, E], F32R)
        neg_half = sb("neg_half", [P, QT])
        eps = sb("eps", [P, QT])

        x_t = sb("x_t", [P, BANKS, EC, S])
        x_s = sb("x_s", [P, BANKS, EC, S], F32R)
        x_n = sb("x_n", [P, QT, E])
        ctx_t = [sb(f"ctx_t{n}", [P, EC, 2 * P]) for n in range(2)]
        ctx_s = sb("ctx_s", [P, 2, EC, 2 * P], F32R)
        ctx_ab = sb("ctx_ab", [P, 2, E])
        m_i = [sb("m_i0", [P, 1, KEYS], I32), sb("m_i1", [P, QT, KEYS], I32)]
        m_bias = [sb("m_bias0", [P, 1, KEYS], BF16), sb("m_bias1", [P, QT, KEYS], BF16)]
        k_s = [sb("k_s0", [P, 2, EC, BANKS, KEYS], F32R), sb("k_s1", [P, 2, EC, KEYS], F32R)]
        k_bd = [sb(f"k_bd{n}", [P, 2, EC, HH, KEYS], F32R) for n in range(2)]
        v_bd = [sb(f"v_bd{n}", [P, 2, 2 * PAIRS, PW]) for n in range(2)]
        neg_max = sb("neg_max", [P, HH])
        diff = sb("diff", [P, HH, KEYS])
        prob = sb("prob", [P, TCOLS])
        prob_t = sb("prob_t", [P, TCOLS])
        rden = sb("rden", [P, 2 * PAIRS, 2])
        att = [sb(f"att{n}", [P, QT, E]) for n in range(2)]
        att_s = [sb(f"att_s{n}", [P, 2, EC, S], F32R) for n in range(2)]
        ysum = [sb(f"ysum{n}", [P, QT, E]) for n in range(3)]
        stats = [sb(f"stats{n}", [P, QT, 6]) for n in range(3)]
        mean_var = [sb(f"mean_var{n}", [P, QT, 2]) for n in range(3)]
        var_eps = [sb(f"var_eps{n}", [P, QT]) for n in range(3)]
        rstd = [sb(f"rstd{n}", [P, QT]) for n in range(3)]
        xhat = [sb(f"xhat{n}", [P, QT, E]) for n in range(3)]
        xn_s = [sb(f"xn_s{n}", [P, 2, EC, S], F32R) for n in range(2)]
        x1_res = sb("x1_res", [P, QT, E])
        h_t = w2
        h_s = sb("h_s", [P, 2, FC, S], F32R)
        x2_res = sb("x2_res", [P, QT, E])
        q_s = sb("q_s", [P, 2, EC, S], F32R)
        o_n = sb("o_n", [P, QT, E])

        p_s = pb("p_s", [P, 2, 512])
        p_t = pb("p_t", [P, 2, 512])
        p_v = pb("p_v", [P, 512])
        ring = [pb(f"ring{n}", [P, 512]) for n in range(3)]
        pt_flat = p_t[:, :, :].rearrange("p a b -> p (a b)")[:, 0:TCOLS]
        pv_all = p_v[:, 0:2 * PAIRS * PW].rearrange("p (j c) -> p j c", c=PW)

        ld_const = sem("ld_const")
        ld_fold = sem("ld_fold")
        ld_side_mask = sem("ld_side_mask")
        ld_v_mask = sem("ld_v_mask")
        ld_wout = sem("ld_wout")
        ld_rows = sem("ld_rows")
        ld_kv1w = sem("ld_kv1w")
        ld_w1 = sem("ld_w1")
        ld_w2 = sem("ld_w2")
        ld_qo1w = sem("ld_qo1w")
        ld_xt = sem("ld_xt")
        ld_xn = sem("ld_xn")
        ld_ctx_t = pair("ld_ctx_t")
        ld_ctx_ab = sem("ld_ctx_ab")
        ld_mask = pair("ld_mask")
        stored = sem("stored")
        ident_b_ready = sem("ident_b_ready")
        pad_ready = sem("pad_ready")
        half_ready = sem("half_ready")
        ones_ready = sem("ones_ready")
        g_mm = sem("g_mm")
        g_ready = sem("g_ready")
        wv_bd_ready = sem("wv_bd_ready")
        wvout_mm = sem("wvout_mm")
        wvout_a_ready = sem("wvout_a_ready")
        wvout_b_ready = sem("wvout_b_ready")
        w1_a_ready = sem("w1_a_ready")
        w1_b_ready = sem("w1_b_ready")
        w2_a_ready = sem("w2_a_ready")
        w2_b_ready = sem("w2_b_ready")
        wq1_a_ready = sem("wq1_a_ready")
        wq1_b_ready = sem("wq1_b_ready")
        wv1_a_ready = sem("wv1_a_ready")
        wv1_b_ready = sem("wv1_b_ready")
        wo1_a_ready = sem("wo1_a_ready")
        wo1_b_ready = sem("wo1_b_ready")
        shift_mm = sem("shift_mm")
        shift_ready = sem("shift_ready")
        k_bd_low_first = sem("k_bd_low_first")
        beta1_ff2_ready = sem("beta1_ff2_ready")
        k_mm = pair("k_mm")
        k_a_ready = pair("k_a_ready")
        k_b_ready = pair("k_b_ready")
        x_a_ready = sem("x_a_ready")
        x_b_ready = sem("x_b_ready")
        k_bd_ready = pair("k_bd_ready")
        ctx_a_ready = sem("ctx_a_ready")
        ctx_b_ready = sem("ctx_b_ready")
        v1_mm = sem("v1_mm")
        v_bd_ready = pair("v_bd_ready")
        bias_ready = pair("bias_ready")
        scores_mm = pair("scores_mm")
        max_ready = pair("max_ready")
        diff_ready = pair("diff_ready")
        prob_ready = pair("prob_ready")
        turned_mm = pair("turned_mm")
        prob_t_ready = pair("prob_t_ready")
        pv_mm = pair("pv_mm")
        rden_ready = pair("rden_ready")
        att_ready = pair("att_ready")
        att_t_mm = pair("att_t_mm")
        att_a_ready = pair("att_a_ready")
        att_b_ready = pair("att_b_ready")
        proj_mm = pair("proj_mm")
        xres_ready = sem("xres_ready")
        y_ready = [sem(f"y_ready{n}") for n in range(3)]
        stats_ready = [sem(f"stats_ready{n}") for n in range(3)]
        mv_ready = [sem(f"mv_ready{n}") for n in range(3)]
        rstd_ready = [sem(f"rstd_ready{n}") for n in range(3)]
        xhat_ready = [sem(f"xhat_ready{n}") for n in range(3)]
        x_t_mm = pair("x_t_mm")
        xn_a_ready = pair("xn_a_ready")
        xn_b_ready = pair("xn_b_ready")
        x1_res_ready = sem("x1_res_ready")
        x2_res_ready = sem("x2_res_ready")
        h_mm = sem("h_mm")
        h_ready = sem("h_ready")
        h_split = sem("h_split")
        ff2_mm = sem("ff2_mm")
        q_mm = sem("q_mm")
        q_a_ready = sem("q_a_ready")
        q_b_ready = sem("q_b_ready")
        o_ready = sem("o_ready")

        block = ctx.enter_context(nc.Block())

        def iterations(eng, body, last_tail):
            body(0, 0, None, None)
            body(1, 1, 0, None)
            with eng.Fori(2, B - 1) as i:
                body(i, i, i - 1, i - 2)
            body(B - 1, B - 1, B - 2, B - 3)
            body(B, None, B - 1, B - 2)
            last_tail(B - 1)

        def more(b):
            return b is not None and not (isinstance(b, int) and b + 1 >= B)

        def later(b):
            return not (isinstance(b, int) and b == 0)

        @block.sync
        def _(sp):
            def of_batch(a, b):
                return a[bass.ds(b * P, P)] if not isinstance(b, int) else a[b * P:b * P + P]

            def load_ctx_t(layer, b):
                sp.dma_start(ctx_t[layer][:], of_batch(d["ctx_t"], b)).then_inc(ld_ctx_t[layer], 16)

            def load_mask(layer, b):
                sp.dma_start(m_i[layer][:], of_batch(d["mask0" if layer == 0 else "mask1"], b)).then_inc(ld_mask[layer], 16)

            sp.dma_start(wk_rep[:], d["wk_rep"]).then_inc(ld_fold, 16)
            sp.dma_start(wq_rep[:], d["wq_rep"]).then_inc(ld_fold, 16)
            sp.dma_start(head_mask[:], d["head_mask"]).then_inc(ld_fold, 16)
            load_ctx_t(0, 0)
            sp.dma_start(side_mask[:], d["side_mask"]).then_inc(ld_side_mask, 16)
            load_mask(0, 0)
            sp.dma_start(v_mask[:], d["v_mask"]).then_inc(ld_v_mask, 16)
            sp.dma_start(ctx_ab[:], of_batch(d["ctx_ab"], 0)).then_inc(ld_ctx_ab, 16)
            sp.dma_start(wv_rep[:], d["wv_rep"]).then_inc(ld_wout, 16)
            sp.dma_start(w_out[:], d["w_out"]).then_inc(ld_wout, 16)
            sp.dma_start(cols[:], d["cols"]).then_inc(ld_rows, 16)
            sp.dma_start(w1[:], d["w1"]).then_inc(ld_w1, 16)
            sp.dma_start(rows[:], d["rows"]).then_inc(ld_rows, 16)
            sp.dma_start(x_n[:], of_batch(d["x_n"], 0)).then_inc(ld_xn, 16)
            sp.dma_start(w2[:], d["w2"]).then_inc(ld_w2, 16)
            sp.dma_start(wq1[:], d["wq1"]).then_inc(ld_qo1w, 16)
            sp.dma_start(wo1[:], d["wo1"]).then_inc(ld_qo1w, 16)
            sp.dma_start(wk1[:], d["wk1"]).then_inc(ld_kv1w, 16)
            sp.dma_start(wv1[:], d["wv1"]).then_inc(ld_kv1w, 16)

            def body(i, b, p, t):
                if more(b):
                    sp.wait_ge(x_b_ready, nth(b, 2, 1))
                    sp.dma_start(x_t[:], of_batch(d["x_t"], b + 1)).then_inc(ld_xt, 16)
                    sp.wait_ge(k_mm[0], nth(b, 1))
                    load_ctx_t(0, b + 1)
                    sp.wait_ge(bias_ready[0], nth(b, 1))
                    load_mask(0, b + 1)
                    sp.wait_ge(v_bd_ready[0], nth(b, 1))
                    sp.dma_start(ctx_ab[:], of_batch(d["ctx_ab"], b + 1)).then_inc(ld_ctx_ab, 16)
                if b is not None:
                    if p is not None:
                        sp.wait_ge(k_mm[1], nth(p, 1))
                        sp.wait_ge(ctx_b_ready, nth(p, 1))
                    load_ctx_t(1, b)
                    if p is not None:
                        sp.wait_ge(bias_ready[1], nth(p, 1))
                    load_mask(1, b)
                if t is not None:
                    sp.wait_ge(o_ready, nth(t, 2, 1))
                    sp.dma_start(of_batch(out, t), o_n[:]).then_inc(stored, 16)
                if more(b):
                    sp.wait_ge(y_ready[0], nth(b, 1))
                    sp.dma_start(x_n[:], of_batch(d["x_n"], b + 1)).then_inc(ld_xn, 16)

            def last_tail(b):
                for qt in range(QT):
                    sp.wait_ge(o_ready, nth(b, 2, qt))
                    sp.dma_start(out[b * P:b * P + P, qt], o_n[:, qt]).then_inc(stored, 16)

            iterations(sp, body, last_tail)
            sp.wait_ge(stored, 16 * (B - 1 + QT))

        @block.tensor
        def _(pe):
            def products(o, lhs, rhs, start, stop):
                for n, (l, r) in enumerate(((0, 0), (0, 1), (1, 0))):
                    last = pe.matmul(o, lhs(l), rhs(r), start=start and n == 0, stop=stop and n == 2)
                return last

            def scores(layer, b, u, before):
                qt, half = u // EC, u % EC
                if u == 0:
                    if layer == 0:
                        pe.wait_ge(x_b_ready, nth(b, 2, 1))
                    pe.wait_ge(bias_ready[layer], nth(b, 1))
                if layer == 1 and qt == 0:
                    pe.wait_ge(q_b_ready, nth(b, EC, half))
                if qt == 0:
                    pe.wait_ge(k_bd_ready[layer], nth(b, 2 * EC, 2 * half + 1))
                    if layer == 0 and not later(b):
                        pe.wait_ge(k_bd_low_first, half + 1)
                for n in range(BANKS):
                    if before is not None:
                        pe.wait_ge(diff_ready[before[0]], nth(before[1], UNITS * BANKS, before[2] * BANKS + n))
                    o = p_s[:, n, 0:BH * KEYS]
                    bias = m_bias[layer][:, qt if layer else 0, :].unsqueeze(1).to_broadcast((P, BH, KEYS))
                    pe.matmul(o, ident_b[:], bias, start=True, stop=False)
                    tile, heads = slice(qt * P, (qt + 1) * P), slice(n * BH, (n + 1) * BH)
                    if layer == 0:
                        for r in range(2):
                            last = pe.matmul(o, x_s[:, n, half, tile], k_bd[0][:, r, half, heads, :], start=False, stop=(r == 1))
                    else:
                        last = products(o, lambda l: q_s[:, l, half, tile], lambda r: k_bd[1][:, r, half, heads, :],
                                        False, True)
                    last.then_inc(scores_mm[layer], 1)

            def turn(layer, b, u, before):
                pe.wait_ge(prob_ready[layer], nth(b, UNITS, u))
                if before is not None:
                    pe.wait_ge(prob_t_ready[before[0]], nth(before[1], UNITS, before[2]))
                for j in range(PAIRS):
                    pe.transpose(p_t[:, 0, j * P:(j + 1) * P], prob[:, j * P:(j + 1) * P], ident[:])
                pe.transpose(p_t[:, 1, 0:P], prob[:, PAIRS * P:], ident[:]).then_inc(turned_mm[layer], 1)

            def values(layer, b, u, before):
                half = u % EC
                pe.wait_ge(prob_t_ready[layer], nth(b, UNITS, u))
                if u == 0:
                    pe.wait_ge(v_bd_ready[layer], nth(b, 1))
                if half == 0 and before is not None:
                    pe.wait_ge(att_ready[before[0]], nth(before[1], QT, before[2] // EC))
                for j in range(PAIRS):
                    pe.matmul(pv_all[:, half * PAIRS + j, :], prob_t[:, j * P:(j + 1) * P],
                              v_bd[layer][:, 0, half * PAIRS + j, :], start=(half == 0 and j == 0), stop=False,
                              skip_group_check=True)
                pe.matmul(pv_all[:, half * PAIRS:(half + 1) * PAIRS, :], prob_t[:, PAIRS * P:],
                          v_bd[layer][:, 1, half * PAIRS:(half + 1) * PAIRS, :], start=False, stop=True,
                          skip_group_check=True).then_inc(pv_mm[layer], 1)

            def keys(layer, b, bank):
                pe.wait_ge(ld_ctx_t[layer], 16 * b + 16)
                c_t = ctx_t[layer][:, :, K_A:K_A + KEYS]
                for m in range(EC):
                    if layer == 0:
                        for n in range(BANKS):
                            last = pe.matmul(bank[:, (m * BANKS + n) * KEYS:(m * BANKS + n + 1) * KEYS],
                                             g_bd[:, n].rearrange("p r c -> p (r c)"), c_t[:, m, :], start=True, stop=True)
                    else:
                        for c in range(EC):
                            last = pe.matmul(bank[:, m * KEYS:(m + 1) * KEYS], wk1[:, c, m * P:(m + 1) * P], c_t[:, c, :],
                                             start=(c == 0), stop=(c == EC - 1))
                last.then_inc(k_mm[layer], 1)

            def values_1(b, part, bank):
                for c in range(EC):
                    last = products(bank[:, part * E:(part + 1) * E], lambda l: ctx_s[:, l, c, part * P:(part + 1) * P],
                                    lambda r: wv1_s[:, r, c, :], c == 0, c == EC - 1)
                last.then_inc(v1_mm, 1)

            def turn_rows(src, bank):
                for c in range(EC):
                    for qt in range(QT):
                        last = pe.transpose(bank[:, c * S + qt * P:c * S + (qt + 1) * P],
                                            src[:, qt, c * P:(c + 1) * P], ident[:])
                return last

            def to_rows(lhs, w, chunks, bank, qt):
                for c in range(chunks):
                    last = products(bank[:, qt * E:(qt + 1) * E], lambda l: lhs[:, l, c, qt * P:(qt + 1) * P],
                                    lambda r: w[:, r, c, :], c == 0, c == chunks - 1)
                return last

            def to_columns(w, m, rhs, o):
                for c in range(EC):
                    last = products(o, lambda l: w[:, l, c, m * P:(m + 1) * P], lambda r: rhs[:, r, c, :],
                                    c == 0, c == EC - 1)
                return last

            def attention_out(layer, b, bank):
                pe.wait_ge(att_ready[layer], nth(b, QT, QT - 1))
                turn_rows(att[layer], bank).then_inc(att_t_mm[layer], 1)

            def project(layer, b, bank):
                pe.wait_ge(att_b_ready[layer], nth(b, 1))
                for qt in range(QT):
                    last = to_rows(att_s[layer], (w_vout_s, wo1_s)[layer], EC, bank, qt)
                last.then_inc(proj_mm[layer], 1)

            def normed_to_columns(n, b, bank):
                pe.wait_ge(xhat_ready[n], nth(b, QT, QT - 1))
                turn_rows(xhat[n], bank).then_inc(x_t_mm[n], 1)

            def ff1(b, g, bank):
                if g == 0:
                    pe.wait_ge(xn_b_ready[0], nth(b, 1))
                for f in (2 * g, 2 * g + 1):
                    last = to_columns(w1_s, f, xn_s[0], bank[:, (f % 2) * S:(f % 2 + 1) * S])
                last.then_inc(h_mm, 1)

            def query_1(b, bank):
                pe.wait_ge(xn_b_ready[1], nth(b, 1))
                for m in range(EC):
                    last = to_columns(wq1_s, m, xn_s[1], bank[:, m * S:(m + 1) * S])
                last.then_inc(q_mm, 1)

            def fold_shift(w, beta, chunks, bank):
                for m in chunks:
                    for c in range(EC):
                        last = pe.matmul(bank[:, m:m + 1], w[:, c, m * P:(m + 1) * P], beta[:, c:c + 1],
                                         start=(c == 0), stop=(c == EC - 1))
                last.then_inc(shift_mm, 1)

            pe.wait_ge(ld_fold, 16 * 3)
            pe.matmul(ring[0][:, 0:P], wk_rep[:], wq_rep[:], start=True, stop=True).then_inc(g_mm, 1)
            pe.wait_ge(g_ready, 1)
            keys(0, 0, ring[2])
            pe.wait_ge(ident_b_ready, 1)
            pe.wait_ge(ld_const, 16)

            def body(i, b, p, t):
                unit = [(0, b, u) if b is not None else None for u in range(UNITS)]
                unit += [(1, p, u) if p is not None else None for u in range(UNITS)]
                older = [(1, t, u) if t is not None else (0, p, u) if p is not None else None for u in (UNITS - 2, UNITS - 1)]
                seq = older + unit

                def s_(s):
                    if unit[s] is not None:
                        scores(*unit[s], seq[s + 1])

                def t_(s):
                    if seq[s + 1] is not None and not (s == 0 and t is None):
                        turn(*seq[s + 1], seq[s])

                def v_(s):
                    if seq[s + 1] is None or (s == 0 and t is None):
                        return
                    tile_before = seq[s] if s else None
                    values(*seq[s + 1], tile_before)

                if p is None and t is None:
                    s_(0)
                    pe.wait_ge(ld_wout, 32)
                    pe.wait_ge(wv_bd_ready, 1)
                    for c in range(EC):
                        last = pe.matmul(ring[1][:, c * E:(c + 1) * E], wv_bd[:], w_out[:, c, :], start=True, stop=True)
                    last.then_inc(wvout_mm, 1)
                    s_(1)
                    t_(1)
                    pe.wait_ge(ld_rows, 32)
                    pe.wait_ge(ld_w1, 16)
                    fold_shift(w1, beta1c, range(0, 1), ring[0])
                    s_(2)
                    v_(1)
                    t_(2)
                    s_(3)
                    v_(2)
                    t_(3)
                    fold_shift(w1, beta1c, range(1, 3), ring[0])
                    v_(3)
                else:
                    s_(0)
                    t_(0)
                    pe.wait_ge(k_b_ready[1], nth(p, 1))
                    ff1(p, 2, ring[1])
                    pe.wait_ge(h_ready, nth(p, FC, 1))
                    ff1(p, 3, ring[2])
                    v_(0)
                    s_(1)
                    t_(1)
                    if not later(p):
                        pe.wait_ge(w2_b_ready, 2)
                    pe.wait_ge(h_split, nth(p, FC, FC - 1))
                    to_rows(h_s, w2_s, FC, ring[0], 0).then_inc(ff2_mm, 1)
                    v_(1)
                    s_(2)
                    t_(2)
                    to_rows(h_s, w2_s, FC, ring[1], 1).then_inc(ff2_mm, 1)
                    if t is not None:
                        attention_out(1, t, ring[2])
                    else:
                        pe.wait_ge(ld_qo1w, 32)
                        fold_shift(wq1, beta2c, range(EC), ring[2])
                    v_(2)
                    s_(3)
                    t_(3)
                if p is not None:
                    pe.wait_ge(y_ready[1], nth(p, QT, QT - 1))
                    if not later(p):
                        pe.wait_ge(wv1_b_ready, 1)
                    pe.wait_ge(ctx_b_ready, nth(p, 1))
                    values_1(p, 0, ring[1])
                    normed_to_columns(1, p, ring[0])
                    v_(3)
                    values_1(p, 1, ring[1])
                t_(4)
                if p is not None:
                    if not later(p):
                        pe.wait_ge(wq1_b_ready, EC)
                    query_1(p, ring[0])
                if more(b):
                    if t is not None:
                        pe.wait_ge(att_b_ready[1], nth(t, 1))
                    elif p is not None:
                        pe.wait_ge(shift_ready, 2)
                    keys(0, b + 1, ring[2])
                v_(4)
                s_(4)
                if b is None:
                    pe.wait_ge(q_b_ready, nth(p, EC, EC - 1))
                    project(1, t, ring[0])
                    s_(5)
                    t_(5)
                    s_(6)
                    v_(5)
                    t_(6)
                    s_(7)
                    v_(6)
                    t_(7)
                    v_(7)
                else:
                    if p is not None:
                        pe.wait_ge(v_bd_ready[1], nth(p, 1))
                    else:
                        pe.wait_ge(wvout_b_ready, 1)
                    attention_out(0, b, ring[1])
                    if not later(b):
                        fold_shift(w1, beta1c, range(3, 5), ring[0])
                    if t is not None:
                        if not later(t):
                            pe.wait_ge(wo1_b_ready, 1)
                        pe.wait_ge(q_b_ready, nth(p, EC, EC - 1))
                        project(1, t, ring[0])
                    s_(5)
                    t_(5)
                    if more(b):
                        pe.wait_ge(k_b_ready[0], nth(b + 1, 1))
                    project(0, b, ring[2])
                    if not later(b):
                        fold_shift(w1, beta1c, range(5, FC), ring[0])
                    v_(5)
                    t_(6)
                    s_(6)
                    v_(6)
                    s_(7)
                    if p is None:
                        pe.wait_ge(shift_ready, 1)
                    normed_to_columns(0, b, ring[0])
                    t_(7)
                    if not later(b):
                        pe.wait_ge(ld_kv1w, 32)
                    keys(1, b, ring[1])
                    v_(7)
                    if not later(b):
                        pe.wait_ge(w1_b_ready, EC)
                    ff1(b, 0, ring[2])
                    ff1(b, 1, ring[0])

            def last_tail(b):
                def turn_tile(qt, bank):
                    pe.wait_ge(att_ready[1], nth(b, QT, qt))
                    for c in range(EC):
                        last = pe.transpose(bank[:, c * P:(c + 1) * P], att[1][:, qt, c * P:(c + 1) * P], ident[:])
                    last.then_inc(att_t_mm[1], 1)

                def project_tile(qt, bank):
                    pe.wait_ge(att_b_ready[1], nth(b, 1, qt))
                    to_rows(att_s[1], wo1_s, EC, bank, qt).then_inc(proj_mm[1], 1)

                turn(1, b, UNITS - 1, (1, b, UNITS - 2))
                pe.wait_ge(y_ready[2], nth(b - 1, 1))
                turn_tile(0, ring[0])
                values(1, b, UNITS - 1, (1, b, UNITS - 2))
                project_tile(0, ring[2])
                turn_tile(1, ring[1])
                project_tile(1, ring[0])

            iterations(pe, body, last_tail)

        @block.vector
        def _(dve):
            def bias_of(layer, b):
                dve.wait_ge(ld_mask[layer], 16 * b + 16)
                dve.tensor_scalar(m_bias[layer][:], m_i[layer][:], float(layer), MASKED, ALU.is_equal, ALU.mult)\
                   .then_inc(bias_ready[layer], 1)

            def flat(a):
                return a.rearrange("p c q -> p (c q)") if len(a.shape) == 3 else a.rearrange("p c n q -> p (c n q)")

            def low_x(b, n):
                dve.wait_ge(x_a_ready, nth(b, 1))
                dst = slice((1 - n) * SIDE, (2 - n) * SIDE)
                dve.tensor_tensor(x_s[dst, n], x_t[dst, n], x_s[dst, n].bitcast(F32), ALU.subtract).then_inc(x_b_ready, 1)

            def low_part(split, src, a_ready, count, done):
                dve.wait_ge(a_ready, count)
                dve.tensor_tensor(flat(split[:, 1]), src, flat(split[:, 0]).bitcast(F32), ALU.subtract).then_inc(done, 1)

            def split(dst, src, done, count):
                dve.tensor_copy(dst[0], src).then_inc(done, 1)
                dve.wait_ge(done, count)
                dve.tensor_tensor(dst[1], src, dst[0].bitcast(F32), ALU.subtract).then_inc(done, 1)

            def low_scaled_weight(split, w, g, c, a_ready, done):
                dve.wait_ge(a_ready, c + 1)
                dve.scalar_tensor_tensor(split[:, 1, c, :], w[:, c, :], g[:, c:c + 1], split[:, 0, c, :].bitcast(F32),
                                         ALU.mult, ALU.subtract).then_inc(done, 1)

            def copy_low_keys_0(c):
                wide = (P, BANKS, BH, KEYS)
                dve.tensor_tensor(k_bd[0][:, 1, c].rearrange("p (n h) k -> p n h k", n=BANKS),
                                  k_s[0][:, 1, c].bitcast(F32).unsqueeze(2).to_broadcast(wide),
                                  side_mask[:].unsqueeze(1).unsqueeze(3).to_broadcast(wide), ALU.mult).then_inc(k_bd_low_first, 1)

            dve.memset(prob[:, HH * K_A:], 0.0).then_inc(pad_ready, 1)
            dve.wait_ge(ld_fold, 16 * 3)
            by_head = head_mask[:].unsqueeze(2).to_broadcast((P, HH, HD))
            dve.wait_ge(g_mm, 1)
            for r in range(2):
                last = dve.tensor_tensor(g_bd[:, :, r].rearrange("p n (h c) -> p n h c", h=BH),
                                         ring[0][:, 0:P].rearrange("p (n h c) -> p n h c", n=BANKS, h=BH),
                                         by_head.rearrange("p (n h) c -> p n h c", n=BANKS), ALU.mult)
            last.then_inc(g_ready, 1)
            dve.wait_ge(ld_const, 16)
            dve.tensor_copy(ident_b[:], ident[:]).then_inc(ident_b_ready, 1)
            bias_of(0, 0)
            for n in range(BANKS):
                low_x(0, n)
            low_part(k_s[0], ring[2][:, 0:EC * BANKS * KEYS], k_a_ready[0], 1, k_b_ready[0])
            dve.wait_ge(ld_side_mask, 16)
            dve.wait_ge(k_b_ready[0], 1)
            for c in range(EC):
                copy_low_keys_0(c)
            dve.wait_ge(ld_wout, 32)
            dve.tensor_tensor(wv_bd[:].rearrange("p (h c) -> p h c", h=HH), wv_rep[:].rearrange("p (h c) -> p h c", h=HH),
                              by_head, ALU.mult).then_inc(wv_bd_ready, 1)
            dve.wait_ge(ld_v_mask, 16)
            for layer in range(2):
                dve.tensor_copy(v_bd[layer][:, :, :, 2 * HD:], v_mask[:, :, :, 2 * HD:]).then_inc(ones_ready, 1)
            dve.wait_ge(ones_ready, 2)

            def shifted(layer, b, u, before):
                four = p_s[:, :, 0:BH * KEYS].rearrange("p n (h k) -> p n h k", h=BH)
                for n in range(BANKS):
                    dve.wait_ge(scores_mm[layer], nth(b, UNITS * BANKS, u * BANKS + n))
                    dve.tensor_reduce(neg_max[:, n * BH:(n + 1) * BH], four[:, n], AX_X, ALU.max, negate=True)\
                       .then_inc(max_ready[layer], 1)
                if before is not None:
                    dve.wait_ge(prob_ready[before[0]], nth(before[1], UNITS, before[2]))
                for n in range(BANKS):
                    dve.wait_ge(max_ready[layer], nth(b, UNITS * BANKS, u * BANKS + n))
                    dve.tensor_tensor(diff[:, n * BH:(n + 1) * BH], four[:, n],
                                      neg_max[:, n * BH:(n + 1) * BH].unsqueeze(2).to_broadcast((P, BH, KEYS)), ALU.add)\
                       .then_inc(diff_ready[layer], 1)

            def normalise(layer, b, qt):
                dve.wait_ge(pv_mm[layer], nth(b, UNITS, qt * EC + EC - 1))
                dve.reciprocal(rden[:], pv_all[:, :, 2 * HD:]).then_inc(rden_ready[layer], 1)
                dve.wait_ge(rden_ready[layer], nth(b, QT, qt))
                dve.tensor_tensor(att[layer][:, qt, :].rearrange("p (j h c) -> p j h c", h=2, c=HD),
                                  pv_all[:, :, 0:2 * HD].rearrange("p j (h c) -> p j h c", h=2),
                                  rden[:].unsqueeze(3).to_broadcast((P, 2 * PAIRS, 2, HD)), ALU.mult)\
                   .then_inc(att_ready[layer], 1)

            def residual_sum(n, b, bank, res):
                dve.tensor_tensor(ysum[n][:].rearrange("p q e -> p (q e)"), bank[:], res[:].rearrange("p q e -> p (q e)"),
                                  ALU.add).then_inc(y_ready[n], 1)

            def statistics(n, b):
                dve.wait_ge(y_ready[n], nth(b, 1))
                for qt in range(QT):
                    dve.bn_stats(stats[n][:, qt, :], ysum[n][:, qt, :]).then_inc(stats_ready[n], 1)
                dve.drain()
                for qt in range(QT):
                    dve.bn_aggr(mean_var[n][:, qt, :], stats[n][:, qt, :]).then_inc(mv_ready[n], 1)

            def sum_and_stats_1(b, qt):
                dve.wait_ge(ff2_mm, nth(b, QT, qt))
                dve.tensor_tensor(ysum[1][:, qt, :], ring[qt][:, qt * E:(qt + 1) * E], x1_res[:, qt, :], ALU.add)\
                   .then_inc(y_ready[1], 1)
                dve.wait_ge(y_ready[1], nth(b, QT, qt))
                dve.bn_stats(stats[1][:, qt, :], ysum[1][:, qt, :]).then_inc(stats_ready[1], 1)
                dve.drain()
                dve.bn_aggr(mean_var[1][:, qt, :], stats[1][:, qt, :]).then_inc(mv_ready[1], 1)

            def normed(n, b):
                dve.wait_ge(rstd_ready[n], nth(b, 2, 1))
                for qt in range(QT):
                    dve.tensor_scalar(xhat[n][:, qt, :], ysum[n][:, qt, :], mean_var[n][:, qt, 0:1],
                                      rstd[n][:, qt:qt + 1], ALU.subtract, ALU.mult).then_inc(xhat_ready[n], 1)

            def split_hidden(b, g):
                dve.wait_ge(h_ready, nth(b, FC, 2 * g + 1))
                split([flat(h_s[:, n, 2 * g:2 * g + 2]) for n in range(2)], flat(h_t[:, 2 * g:2 * g + 2]),
                      h_split, nth(b, FC, 2 * g))

            def low_query(b, bank):
                dve.wait_ge(q_a_ready, nth(b, 1))
                for m in range(EC):
                    dve.scalar_tensor_tensor(q_s[:, 1, m, :], bank[:, m * S:(m + 1) * S], q_shift[:, m:m + 1],
                                             q_s[:, 0, m, :].bitcast(F32), ALU.add, ALU.subtract).then_inc(q_b_ready, 1)

            def body(i, b, p, t):
                unit = [(0, b, u) if b is not None else None for u in range(UNITS)]
                unit += [(1, p, u) if p is not None else None for u in range(UNITS)]
                seq = [(1, t, UNITS - 1) if t is not None else (0, p, UNITS - 1) if p is not None else None] + unit

                def d_(s):
                    if unit[s] is not None:
                        shifted(*unit[s], seq[s])

                if p is not None:
                    split_hidden(p, 0)
                d_(0)
                if p is not None:
                    split_hidden(p, 1)
                    split_hidden(p, 2)
                if p is not None:
                    split_hidden(p, 3)
                d_(1)
                if not later(b):
                    low_part(w_vout_s, ring[1][:], wvout_a_ready, 1, wvout_b_ready)
                if t is not None:
                    normalise(1, t, 1)
                if p is not None:
                    if later(p):
                        dve.wait_ge(scores_mm[1], nth(p - 1, UNITS * BANKS, UNITS * BANKS - 1))
                    bias_of(1, p)
                if p is not None:
                    dve.wait_ge(x1_res_ready, nth(p, 2, 1))
                    sum_and_stats_1(p, 0)
                d_(2)
                if p is not None:
                    sum_and_stats_1(p, 1)
                if t is not None:
                    low_part(att_s[1], ring[2][:], att_a_ready[1], nth(t, 1), att_b_ready[1])
                if p is not None:
                    if b is not None:
                        normalise(0, b, 0)
                    if later(p):
                        dve.wait_ge(x2_res_ready, nth(p - 1, 2, 1))
                    normed(1, p)
                    if t is None:
                        dve.wait_ge(shift_mm, 5)
                        dve.tensor_copy(q_shift, ring[2][:, 0:EC]).then_inc(shift_ready, 1)
                d_(3)
                if p is None and b is not None:
                    normalise(0, b, 0)
                    for c in range(EC):
                        low_scaled_weight(w1_s, w1, g1c, c, w1_a_ready, w1_b_ready)
                if p is not None:
                    low_part(xn_s[1], ring[0][:], xn_a_ready[1], nth(p, 1), xn_b_ready[1])
                if more(b):
                    for n in range(BANKS):
                        low_x(b + 1, n)
                if p is not None:
                    dve.wait_ge(v1_mm, nth(p, 2, 1))
                    dve.tensor_tensor(v_bd[1][:, :, :, 0:2 * HD], ring[1][:].rearrange("p (a j c) -> p a j c", a=2, c=2 * HD),
                                      v_mask[:, :, :, 0:2 * HD], ALU.mult).then_inc(v_bd_ready[1], 1)
                    low_query(p, ring[0])
                if b is not None:
                    normalise(0, b, 1)
                d_(4)
                if more(b):
                    low_part(k_s[0], ring[2][:, 0:EC * BANKS * KEYS], k_a_ready[0], nth(b + 1, 1), k_b_ready[0])
                    dve.wait_ge(scores_mm[0], nth(b, UNITS * BANKS, UNITS * BANKS - 1))
                    bias_of(0, b + 1)
                if b is not None:
                    low_part(att_s[0], ring[1][:], att_a_ready[0], nth(b, 1), att_b_ready[0])
                d_(5)
                if b is not None:
                    dve.wait_ge(proj_mm[0], nth(b, 1))
                    dve.wait_ge(xres_ready, nth(b, 1))
                    residual_sum(0, b, ring[2], x_n)
                    statistics(0, b)
                if t is not None:
                    dve.wait_ge(proj_mm[1], nth(t, 1))
                    dve.wait_ge(x2_res_ready, nth(t, 2, 1))
                    residual_sum(2, t, ring[0], x2_res)
                if not later(b):
                    dve.wait_ge(shift_mm, 4)
                    dve.tensor_tensor(h_shift, ring[0][:, 0:FC], b_ff1c, ALU.add).then_inc(shift_ready, 1)
                d_(6)
                if b is not None:
                    normed(0, b)
                if not later(b):
                    for c in range(EC):
                        low_scaled_weight(wq1_s, wq1, g2c, c, wq1_a_ready, wq1_b_ready)
                if p is not None and b is not None:
                    normalise(1, p, 0)
                if t is not None:
                    statistics(2, t)
                if b is not None:
                    low_part(xn_s[0], ring[0][:], xn_a_ready[0], nth(b, 1), xn_b_ready[0])
                d_(7)
                if p is not None and b is None:
                    normalise(1, p, 0)
                if t is not None:
                    if later(t):
                        dve.wait_ge(o_ready, nth(t - 1, 2, 1))
                    normed(2, t)
                if b is not None:
                    low_part(k_s[1], ring[1][:, 0:EC * KEYS], k_a_ready[1], nth(b, 1), k_b_ready[1])

            def last_tail(b):
                def low_tile(qt, bank):
                    dve.wait_ge(att_a_ready[1], nth(b, 1, qt))
                    tile = slice(qt * P, (qt + 1) * P)
                    dve.tensor_tensor(att_s[1][:, 1, :, tile], bank[:, 0:EC * P].rearrange("p (c q) -> p c q", c=EC),
                                      att_s[1][:, 0, :, tile].bitcast(F32), ALU.subtract).then_inc(att_b_ready[1], 1)

                def sum_tile(qt, bank):
                    dve.wait_ge(proj_mm[1], nth(b, 1, qt))
                    dve.tensor_tensor(ysum[2][:, qt, :], bank[:, qt * E:(qt + 1) * E], x2_res[:, qt, :], ALU.add)\
                       .then_inc(y_ready[2], 1)
                    dve.wait_ge(y_ready[2], nth(b, 1, qt))
                    dve.bn_stats(stats[2][:, qt, :], ysum[2][:, qt, :]).then_inc(stats_ready[2], 1)
                    dve.drain()
                    dve.bn_aggr(mean_var[2][:, qt, :], stats[2][:, qt, :]).then_inc(mv_ready[2], 1)

                def output_tile(qt):
                    dve.scalar_tensor_tensor(xhat[2][:, qt, :], ysum[2][:, qt, :], mean_var[2][:, qt, 0:1], gamma_r,
                                             ALU.subtract, ALU.mult).then_inc(xhat_ready[2], 1)
                    dve.wait_ge(xhat_ready[2], nth(b, QT, qt))
                    dve.wait_ge(rstd_ready[2], nth(b, 2, 2 * qt + 1))
                    dve.wait_ge(stored, 16 * b)
                    dve.scalar_tensor_tensor(o_n[:, qt, :], xhat[2][:, qt, :], rstd[2][:, qt:qt + 1], beta_r,
                                             ALU.mult, ALU.add).then_inc(o_ready, 1)

                low_tile(0, ring[0])
                normalise(1, b, 1)
                dve.wait_ge(x2_res_ready, nth(b, 2, 1))
                dve.wait_ge(o_ready, nth(b - 1, 2, 1))
                low_tile(1, ring[1])
                sum_tile(0, ring[2])
                dve.wait_ge(mv_ready[2], nth(b, QT, 0))
                output_tile(0)
                sum_tile(1, ring[0])
                dve.wait_ge(mv_ready[2], nth(b, QT, 1))
                output_tile(1)

            iterations(dve, body, last_tail)

        @block.scalar
        def _(act):
            def exponential(layer, b, u, before):
                act.wait_ge(diff_ready[layer], nth(b, UNITS * BANKS, u * BANKS + 1))
                if before is not None:
                    act.wait_ge(turned_mm[before[0]], nth(before[1], UNITS, before[2]))
                act.activation(prob[:, 0:HH * K_A].rearrange("p (h k) -> p h k", h=HH), diff[:, :, 0:K_A], ACT.Exp,
                               scale=SCALE[layer])
                act.activation(prob[:, HH * K_A:].rearrange("p (h k) -> p h k", h=HH)[:, :, 0:KEYS - K_A],
                               diff[:, :, K_A:], ACT.Exp, scale=SCALE[layer]).then_inc(prob_ready[layer], 1)

            def copy_turned(layer, b, u, before):
                act.wait_ge(turned_mm[layer], nth(b, UNITS, u))
                if before is not None:
                    act.wait_ge(pv_mm[before[0]], nth(before[1], UNITS, before[2]))
                act.activation(prob_t[:], pt_flat, ACT.Copy).then_inc(prob_t_ready[layer], 1)

            def high_part(split, src, produced, count, done):
                act.wait_ge(produced, count)
                a = split[:, 0]
                act.activation(a.rearrange("p c q -> p (c q)") if len(a.shape) == 3 else a.rearrange("p c n q -> p (c n q)"),
                               src, ACT.Copy).then_inc(done, 1)

            def high_x(b):
                act.wait_ge(ld_xt, 16 * b + 16)
                act.activation(x_s[:].rearrange("p n c q -> p (n c q)"), x_t[:].rearrange("p n c q -> p (n c q)"), ACT.Copy)\
                   .then_inc(x_a_ready, 1)

            def high_query(b, bank):
                act.wait_ge(q_mm, nth(b, 1))
                if not later(b):
                    act.wait_ge(shift_ready, 2)
                for m in range(EC):
                    last = act.activation(q_s[:, 0, m, :], bank[:, m * S:(m + 1) * S], ACT.Identity, bias=q_shift[:, m:m + 1])
                last.then_inc(q_a_ready, 1)

            def high_scaled_weight(split, w, g, c, done):
                act.activation(split[:, 0, c, :], w[:, c, :], ACT.Copy, scale=g[:, c:c + 1]).then_inc(done, 1)

            def hidden(b, g, bank):
                act.wait_ge(h_mm, nth(b, FC // 2, g))
                for f in (2 * g, 2 * g + 1):
                    act.activation(h_t[:, f, :], bank[:, (f % 2) * S:(f % 2 + 1) * S], ACT.Relu,
                                   bias=h_shift[:, f:f + 1]).then_inc(h_ready, 1)

            act.dma_start(x_t[:], d["x_t"][0:P]).then_inc(ld_xt, 16)
            act.dma_start(ident[:], d["ident"]).then_inc(ld_const, 16)
            high_x(0)
            high_part(k_s[0], ring[2][:, 0:EC * BANKS * KEYS], k_mm[0], 1, k_a_ready[0])
            act.wait_ge(pad_ready, 1)

            def body(i, b, p, t):
                unit = [(0, b, u) if b is not None else None for u in range(UNITS)]
                unit += [(1, p, u) if p is not None else None for u in range(UNITS)]
                older = [(1, t, u) if t is not None else (0, p, u) if p is not None else None for u in (UNITS - 2, UNITS - 1)]
                seq = older + unit

                def c_(s):
                    if seq[s + 1] is not None and not (s == 0 and t is None):
                        copy_turned(*seq[s + 1], seq[s])

                def e_(s):
                    if unit[s] is not None:
                        exponential(*unit[s], seq[s + 1])

                if p is not None:
                    if not later(p):
                        act.wait_ge(shift_ready, 1)
                        act.wait_ge(w2_b_ready, 2)
                    hidden(p, 0, ring[2])
                    hidden(p, 1, ring[0])
                c_(0)
                e_(0)
                if not later(b):
                    high_part(w_vout_s, ring[1][:], wvout_mm, 1, wvout_a_ready)
                if p is not None:
                    hidden(p, 2, ring[1])
                    hidden(p, 3, ring[2])
                c_(1)
                e_(1)
                if not later(b):
                    act.wait_ge(ld_rows, 32)
                    act.wait_ge(ld_w1, 16)
                    high_scaled_weight(w1_s, w1, g1c, 0, w1_a_ready)
                if p is not None:
                    act.wait_ge(ld_ctx_t[1], 16 * p + 16)
                    if later(p):
                        act.wait_ge(v1_mm, nth(p - 1, 2, 1))
                    act.activation(ctx_s[:, 0], ctx_t[1][:], ACT.Copy).then_inc(ctx_a_ready, 1)
                c_(2)
                if t is not None:
                    high_part(att_s[1], ring[2][:], att_t_mm[1], nth(t, 1), att_a_ready[1])
                e_(2)
                if not later(b):
                    high_scaled_weight(w1_s, w1, g1c, 1, w1_a_ready)
                c_(3)
                if p is not None:
                    high_part(xn_s[1], ring[0][:], x_t_mm[1], nth(p, 1), xn_a_ready[1])
                e_(3)
                if not later(b):
                    act.wait_ge(ld_w2, 16)
                    act.activation(w2_s[:, 0, 0:FC // 2], w2[:, 0:FC // 2], ACT.Copy).then_inc(w2_a_ready, 1)
                if more(b):
                    act.wait_ge(scores_mm[0], nth(b, UNITS * BANKS, UNITS * BANKS - 1))
                    high_x(b + 1)
                c_(4)
                if p is not None:
                    high_query(p, ring[0])
                if more(b):
                    high_part(k_s[0], ring[2][:, 0:EC * BANKS * KEYS], k_mm[0], nth(b + 1, 1), k_a_ready[0])
                if not later(b):
                    act.activation(w2_s[:, 0, FC // 2:], w2[:, FC // 2:], ACT.Copy).then_inc(w2_a_ready, 1)
                if b is not None:
                    high_part(att_s[0], ring[1][:], att_t_mm[0], nth(b, 1), att_a_ready[0])
                e_(4)
                c_(5)
                e_(5)
                c_(6)
                e_(6)
                if not later(b):
                    act.wait_ge(ld_qo1w, 32)
                    for c in range(EC):
                        high_scaled_weight(wq1_s, wq1, g2c, c, wq1_a_ready)
                    act.activation(wo1_s[:, 0], wo1[:], ACT.Copy).then_inc(wo1_a_ready, 1)
                    act.wait_ge(ld_kv1w, 32)
                    act.activation(wv1_s[:, 0], wv1[:], ACT.Copy).then_inc(wv1_a_ready, 1)
                if b is not None:
                    high_part(xn_s[0], ring[0][:], x_t_mm[0], nth(b, 1), xn_a_ready[0])
                c_(7)
                if b is not None:
                    high_part(k_s[1], ring[1][:, 0:EC * KEYS], k_mm[1], nth(b, 1), k_a_ready[1])
                e_(7)

            def last_tail(b):
                def high_tile(qt, bank):
                    act.wait_ge(att_t_mm[1], nth(b, 1, qt))
                    act.activation(att_s[1][:, 0, :, qt * P:(qt + 1) * P],
                                   bank[:, 0:EC * P].rearrange("p (c q) -> p c q", c=EC), ACT.Copy).then_inc(att_a_ready[1], 1)

                copy_turned(1, b, UNITS - 1, (1, b, UNITS - 2))
                high_tile(0, ring[0])
                high_tile(1, ring[1])

            iterations(act, body, last_tail)

        @block.gpsimd
        def _(pool):
            def block_keys(layer, b):
                wide = (P, BANKS, BH, KEYS)
                first = layer == 0 and not later(b)
                for c in range(EC):
                    for n in range(2 - first):
                        if c == 0:
                            pool.wait_ge((k_a_ready, k_b_ready)[n][layer], nth(b, 1))
                        if layer == 0:
                            last = pool.tensor_tensor(k_bd[0][:, n, c].rearrange("p (n h) k -> p n h k", n=BANKS),
                                                      k_s[0][:, n, c].bitcast(F32).unsqueeze(2).to_broadcast(wide),
                                                      side_mask[:].unsqueeze(1).unsqueeze(3).to_broadcast(wide), ALU.mult)
                        else:
                            last = pool.tensor_tensor(k_bd[1][:, n, c],
                                                      k_s[1][:, n, c].bitcast(F32).unsqueeze(1).to_broadcast((P, HH, KEYS)),
                                                      head_mask[:].unsqueeze(2).to_broadcast((P, HH, KEYS)), ALU.mult)
                        last.then_inc(k_bd_ready[layer], 1 + first)

            def block_values_0(b):
                pool.wait_ge(ld_ctx_ab, 16 * b + 16)
                pool.tensor_tensor(v_bd[0][:, :, :, 0:2 * HD], ctx_ab[:].rearrange("p a (j c) -> p a j c", c=2 * HD),
                                   v_mask[:, :, :, 0:2 * HD], ALU.mult).then_inc(v_bd_ready[0], 1)

            def inverse_deviation(n, b):
                pool.wait_ge(mv_ready[n], nth(b, QT, QT - 1))
                pool.tensor_tensor(var_eps[n][:], mean_var[n][:, :, 1], eps[:], ALU.add).then_inc(rstd_ready[n], 1)
                pool.wait_ge(rstd_ready[n], nth(b, 2, 0))
                pool.tensor_tensor(rstd[n][:], var_eps[n][:], neg_half[:], ALU.pow).then_inc(rstd_ready[n], 1)

            def gain_and_shift(n, b, dst, g, shift, done):
                pool.wait_ge(xhat_ready[n], nth(b, QT, QT - 1))
                wide = (P, QT, E)
                pool.tensor_tensor(dst[:], xhat[n][:], g.unsqueeze(1).to_broadcast(wide), ALU.mult).then_inc(done, 1)
                pool.wait_ge(done, nth(b, 2, 0))
                pool.tensor_tensor(dst[:], dst[:], shift.unsqueeze(1).to_broadcast(wide), ALU.add).then_inc(done, 1)

            pool.memset(neg_half[:], -0.5).then_inc(half_ready, 1)
            pool.memset(eps[:], EPS).then_inc(half_ready, 1)
            pool.wait_ge(half_ready, 2)
            pool.wait_ge(ld_side_mask, 16)
            block_keys(0, 0)
            pool.wait_ge(ld_v_mask, 16)
            pool.wait_ge(ones_ready, 2)
            block_values_0(0)
            pool.wait_ge(ld_rows, 32)
            pool.tensor_tensor(beta1_ff2_r[:], beta1_r, b_ff2_r, ALU.add).then_inc(beta1_ff2_ready, 1)
            pool.wait_ge(beta1_ff2_ready, 1)

            def body(i, b, p, t):
                if p is not None:
                    if later(p):
                        pool.wait_ge(scores_mm[1], nth(p - 1, UNITS * BANKS, UNITS * BANKS - 1))
                    block_keys(1, p)
                if b is not None:
                    pool.wait_ge(ld_xn, 16 * b + 16)
                    pool.tensor_tensor(x_n[:], x_n[:], b_out_r.unsqueeze(1).to_broadcast((P, QT, E)), ALU.add)\
                        .then_inc(xres_ready, 1)
                if not later(b):
                    for n in range(2):
                        chunks = slice(n * FC // 2, (n + 1) * FC // 2)
                        pool.wait_ge(w2_a_ready, n + 1)
                        pool.tensor_tensor(w2_s[:, 1, chunks], w2[:, chunks], w2_s[:, 0, chunks].bitcast(F32), ALU.subtract)\
                            .then_inc(w2_b_ready, 1)
                if p is not None:
                    pool.wait_ge(ctx_a_ready, nth(p, 1))
                    pool.tensor_tensor(ctx_s[:, 1], ctx_t[1][:], ctx_s[:, 0].bitcast(F32), ALU.subtract).then_inc(ctx_b_ready, 1)
                if p is not None:
                    inverse_deviation(1, p)
                if more(b):
                    pool.wait_ge(scores_mm[0], nth(b, UNITS * BANKS, UNITS * BANKS - 1))
                    block_keys(0, b + 1)
                if b is not None:
                    inverse_deviation(0, b)
                if more(b):
                    pool.wait_ge(pv_mm[0], nth(b, UNITS, UNITS - 1))
                    block_values_0(b + 1)
                if t is not None:
                    inverse_deviation(2, t)
                if p is not None:
                    if later(p):
                        pool.wait_ge(y_ready[2], nth(p - 1, 1))
                    gain_and_shift(1, p, x2_res, g2_r, beta2_r, x2_res_ready)
                if b is not None:
                    if p is not None:
                        pool.wait_ge(y_ready[1], nth(p, QT, QT - 1))
                    gain_and_shift(0, b, x1_res, g1_r, beta1_ff2_r[:], x1_res_ready)
                if not later(b):
                    pool.wait_ge(wo1_a_ready, 1)
                    pool.tensor_tensor(wo1_s[:, 1], wo1[:], wo1_s[:, 0].bitcast(F32), ALU.subtract).then_inc(wo1_b_ready, 1)
                    pool.wait_ge(wv1_a_ready, 1)
                    pool.tensor_tensor(wv1_s[:, 1], wv1[:], wv1_s[:, 0].bitcast(F32), ALU.subtract).then_inc(wv1_b_ready, 1)
                if t is not None:
                    if later(t):
                        pool.wait_ge(stored, 16 * t)
                    gain_and_shift(2, t, o_n, gamma_r, beta_r, o_ready)

            def last_tail(b):
                for qt in range(QT):
                    pool.wait_ge(mv_ready[2], nth(b, QT, qt))
                    pool.tensor_tensor(var_eps[2][:, qt:qt + 1], mean_var[2][:, qt, 1:2], eps[:, qt:qt + 1], ALU.add)\
                        .then_inc(rstd_ready[2], 1)
                    pool.wait_ge(rstd_ready[2], nth(b, 2, 2 * qt))
                    pool.tensor_tensor(rstd[2][:, qt:qt + 1], var_eps[2][:, qt:qt + 1], neg_half[:, qt:qt + 1], ALU.pow)\
                        .then_inc(rstd_ready[2], 1)

            iterations(pool, body, last_tail)


def kernel(**inputs):
    import numpy as np
    import concourse.bacc as bacc
    from concourse import mybir as mb
    from concourse.bass_utils import run_bass_kernel_spmd

    a = {k: np.asarray(v) for k, v in inputs.items()}
    x, c = a["x"], a["ctx_1024"]

    def chunks(w):
        return w.reshape(-1, P, w.shape[1]).transpose(1, 0, 2)

    def by_batch(w):
        return w.reshape(B, -1, P, w.shape[2]).transpose(0, 2, 1, 3).reshape(B * P, -1, w.shape[2])

    c_ab = np.zeros((B, P, 2, E), c.dtype)
    c_ab[:, :, 0] = np.tile(c[:, :K_A], (1, 2, 1))
    tail = np.zeros((B, K_B, E), c.dtype)
    tail[:, :KEYS - K_A] = c[:, K_A:]
    c_ab[:, :, 1] = np.tile(tail, (1, HH, 1))

    row = np.arange(P)
    head_mask = (row[:, None] // HD == np.arange(HH)[None, :]).astype(np.float32)
    in_pair = np.concatenate([np.arange(2 * HD) // HD, np.arange(2)])
    v_mask = np.zeros((P, 2, 2 * PAIRS, PW), np.float32)
    v_mask[:, 0] = (in_pair[None, None, :] == (row // K_A)[:, None, None])
    head = 2 * (np.arange(2 * PAIRS) % PAIRS)[:, None] + in_pair[None, :]
    v_mask[:, 1] = (head[None] == (row // K_B)[:, None, None]) & ((row % K_B) < KEYS - K_A)[:, None, None]

    vectors = ("b_out", "g1", "beta1", "b_ff2", "g2", "beta2")
    row_vectors = [a[f"L0_xattn_{n}"] for n in vectors] + [a["L1_xattn_gamma"], a["L1_xattn_beta"]]
    col_vectors = [a[f"L0_xattn_{n}"].reshape(-1, P).T for n in ("g1", "beta1", "g2", "beta2", "b_ff1")]
    x_t = np.stack([x.transpose(0, 2, 1).reshape(B, EC, BANKS, SIDE, S).transpose(0, 3, 2, 1, 4)] * 2, axis=1)
    arrays = {
        "x_t": x_t.reshape(B * P, BANKS, EC, S),
        "x_n": by_batch(x),
        "ctx_t": by_batch(c_ab.transpose(0, 3, 2, 1).reshape(B, E, 2 * P)),
        "ctx_ab": c_ab.reshape(B * P, 2, E),
        "mask0": np.broadcast_to(a["mask_Bx1x1xS2_if1"][:, 0], (B, P, KEYS)).reshape(B * P, 1, KEYS),
        "mask1": by_batch(a["mask_BxSxS2_ik1"]),
        "ident": np.eye(P, dtype=np.float32),
        "head_mask": head_mask,
        "side_mask": (row[:, None] % SIDE // HD == np.arange(BH)[None, :]).astype(np.float32),
        "v_mask": v_mask,
        "rows": np.broadcast_to(np.stack(row_vectors)[None], (P, 8, E)),
        "cols": np.concatenate(col_vectors, axis=1),
        "wk_rep": np.tile(a["L0_xattn_wk"].T, (1, HH)),
        "wq_rep": np.tile(a["L0_xattn_wq"].T, (1, HH)),
        "wv_rep": np.tile(a["L0_xattn_wv"].T, (HH, HH)),
        "w_out": chunks(a["L0_xattn_w_out"]),
        "w1": chunks(a["L0_xattn_w_ff1"]),
        "w2": chunks(a["L0_xattn_w_ff2"]),
        "wq1": chunks(a["L1_xattn_W_Q"].T),
        "wk1": chunks(a["L1_xattn_W_K"].T),
        "wv1": chunks(a["L1_xattn_W_V"].T),
        "wo1": chunks(a["L1_xattn_W_O"].T),
    }
    arrays = {f"in_{k}": np.ascontiguousarray(v) for k, v in arrays.items()}
    nc = bacc.Bacc("TRN2", target_bir_lowering=False, num_devices=1)
    d = {k[3:]: nc.dram_tensor(k, v.shape, mb.dt.from_np(v.dtype), kind="ExternalInput").ap() for k, v in arrays.items()}
    out = nc.dram_tensor("out", (B * P, QT, E), F32, kind="ExternalOutput").ap()
    build(nc, d, out)
    r = run_bass_kernel_spmd(nc, [arrays], core_ids=[0])
    o = r.results[0]["out"]
    return o.reshape(B, P, QT, E).transpose(0, 2, 1, 3).reshape(B, S, E)
```
